# Optimizing a Trainium2 kernel written in Bass

```python
import numpy as np
import jax
import jax.numpy as jnp

def _softmax(x, axis=-1):
    return jax.nn.softmax(x, axis=axis)

def _gelu(x):
    return jax.nn.gelu(x, approximate=True)

def _silu(x):
    return jax.nn.silu(x)

def _sigmoid(x):
    return jax.nn.sigmoid(x)

def _layernorm(x, axis=-1, eps=1e-05):
    m = jnp.mean(x, axis=axis, keepdims=True)
    v = jnp.var(x, axis=axis, keepdims=True)
    return (x - m) / jnp.sqrt(v + eps)

def _scatter_add(tgt, idx, src, axis=0):
    return tgt.at[idx].add(src)

def _segment_sum(src, seg, n):
    return jax.ops.segment_sum(src, seg, n)
kernel_name = 'mk_adj_ffn_d1_adj_r2_003ea9'

def setup_inputs(seed: int=0):
    np.random.seed(seed)
    _w = jnp.asarray

    def _rec_inputs():
        import jax
        import jax.numpy as jnp
        _gk = jax.random.key(seed)
        x = -0.0002928 + 1 * jax.random.normal(jax.random.fold_in(_gk, 1), (128, 128, 128), jnp.float32)
        _a = jax.random.bernoulli(jax.random.fold_in(_gk, 2), 0.03125, (128, 128, 128))
        _a = jnp.logical_or(_a, jnp.swapaxes(_a, -1, -2))
        _a = jnp.logical_or(_a, jnp.eye(128, dtype=bool))
        _af = _a.astype(jnp.float32)
        _af = _af * jax.random.uniform(jax.random.fold_in(_gk, 3), (128, 128, 128), jnp.float32, 0.05, 1)
        adj = _af
        return (x, adj)
    x, adj = _rec_inputs()

    def _L0_gnn_setup():
        import jax, jax.numpy as jnp
        import numpy as np
        B, N, D, H = (8, 1024, 128, 512)
        RMS_EPS = 1e-06

        def _rmsnorm(h, w, eps=RMS_EPS):
            var = jnp.mean(jnp.square(h), axis=-1, keepdims=True)
            return h * jax.lax.rsqrt(var + eps) * w
        key = jax.random.key(seed)
        ks = jax.random.split(key, 5)
        x = jax.random.normal(ks[0], (B, N, D), dtype=jnp.float32)
        adjacency = jax.random.uniform(ks[1], (B, N, N), dtype=jnp.float32)
        epsilon = jnp.zeros((), dtype=jnp.float32)
        W1 = jax.random.normal(ks[2], (D, H), dtype=jnp.float32) * (1.0 / np.sqrt(D))
        b1 = jnp.zeros((H,), dtype=jnp.float32)
        rms_weight = jnp.ones((H,), dtype=jnp.float32)
        W2 = jax.random.normal(ks[3], (H, D), dtype=jnp.float32) * (1.0 / np.sqrt(H))
        b2 = jnp.zeros((D,), dtype=jnp.float32)
        return {'x': x, 'adjacency': adjacency, 'epsilon': epsilon, 'W1': W1, 'b1': b1, 'rms_weight': rms_weight, 'W2': W2, 'b2': b2}
    _L0_gnn_all = _L0_gnn_setup()
    _L0_gnn_in = {k: v for k, v in _L0_gnn_all.items() if k in ('epsilon', 'W1', 'b1', 'rms_weight', 'W2', 'b2')}
    del _L0_gnn_all

    def _L0_ffn_setup():
        import jax, jax.numpy as jnp
        import numpy as np
        B, T, C = (64, 192, 128)
        NH, NKV = (4, 2)
        HD = C // NH
        NREP = NH // NKV
        NE, TOPK = (8, 2)
        HID = int(8 / 3 * C)
        EPS_RMS = 1e-06

        def _rope_tables(t_len):
            inv_freq = 1.0 / 10000.0 ** (np.arange(0, HD, 2, dtype=np.float32) / HD)
            t = np.arange(t_len, dtype=np.float32)
            freqs = np.outer(t, inv_freq)
            emb = np.concatenate([freqs, freqs], axis=-1)
            return (jnp.asarray(np.cos(emb)), jnp.asarray(np.sin(emb)))

        def _rotate_half(x):
            h = x.shape[-1] // 2
            return jnp.concatenate([-x[..., h:], x[..., :h]], axis=-1)

        def _rmsnorm(v, w):
            return v * jax.lax.rsqrt(jnp.mean(v * v, axis=-1, keepdims=True) + EPS_RMS) * w
        key = jax.random.key(seed)
        ks = jax.random.split(key, 10)
        s = lambda k, shape: jax.random.normal(k, shape, jnp.float32) * 0.02
        return {'x': jax.random.normal(ks[0], (B, T, C), jnp.float32), 'ln1_w': jnp.ones((C,), jnp.float32), 'ln2_w': jnp.ones((C,), jnp.float32), 'wq': s(ks[1], (NH * HD, C)), 'wk': s(ks[2], (NKV * HD, C)), 'wv': s(ks[3], (NKV * HD, C)), 'wo': s(ks[4], (C, C)), 'router_w': s(ks[5], (NE, C)), 'w1': s(ks[6], (NE, HID, C)), 'w2': s(ks[7], (NE, C, HID)), 'w3': s(ks[8], (NE, HID, C))}
    _L0_ffn_all = _L0_ffn_setup()
    _L0_ffn_in = {k: v for k, v in _L0_ffn_all.items() if k in ('ln1_w', 'ln2_w', 'wq', 'wk', 'wv', 'wo', 'router_w', 'w1', 'w2', 'w3')}
    del _L0_ffn_all
    return {'x': x, 'adj': adj, 'L0_gnn_epsilon': _L0_gnn_in['epsilon'], 'L0_gnn_W1': _L0_gnn_in['W1'], 'L0_gnn_b1': _L0_gnn_in['b1'], 'L0_gnn_rms_weight': _L0_gnn_in['rms_weight'], 'L0_gnn_W2': _L0_gnn_in['W2'], 'L0_gnn_b2': _L0_gnn_in['b2'], 'L0_ffn_ln1_w': _L0_ffn_in['ln1_w'], 'L0_ffn_ln2_w': _L0_ffn_in['ln2_w'], 'L0_ffn_wq': _L0_ffn_in['wq'], 'L0_ffn_wk': _L0_ffn_in['wk'], 'L0_ffn_wv': _L0_ffn_in['wv'], 'L0_ffn_wo': _L0_ffn_in['wo'], 'L0_ffn_router_w': _L0_ffn_in['router_w'], 'L0_ffn_w1': _L0_ffn_in['w1'], 'L0_ffn_w2': _L0_ffn_in['w2'], 'L0_ffn_w3': _L0_ffn_in['w3']}

def reference(x, adj, L0_gnn_epsilon, L0_gnn_W1, L0_gnn_b1, L0_gnn_rms_weight, L0_gnn_W2, L0_gnn_b2, L0_ffn_ln1_w, L0_ffn_ln2_w, L0_ffn_wq, L0_ffn_wk, L0_ffn_wv, L0_ffn_wo, L0_ffn_router_w, L0_ffn_w1, L0_ffn_w2, L0_ffn_w3):
    import jax
    import jax.numpy as jnp

    def _L0_gnn_ref(x, adjacency, epsilon, W1, b1, rms_weight, W2, b2):
        import jax, jax.numpy as jnp
        import numpy as np
        B, N, D, H = (8, 1024, 128, 512)
        RMS_EPS = 1e-06

        def _rmsnorm(h, w, eps=RMS_EPS):
            var = jnp.mean(jnp.square(h), axis=-1, keepdims=True)
            return h * jax.lax.rsqrt(var + eps) * w
        neighbor_sum = jnp.einsum('bnm,bmd->bnd', adjacency, x)
        agg = epsilon * x + neighbor_sum
        h = jnp.einsum('bnd,dh->bnh', agg, W1) + b1
        h = jax.nn.silu(_rmsnorm(h, rms_weight))
        out = jnp.einsum('bnh,hd->bnd', h, W2) + b2
        return out

    def _L0_ffn_ref(x, ln1_w, ln2_w, wq, wk, wv, wo, router_w, w1, w2, w3):
        import jax, jax.numpy as jnp
        import numpy as np
        B, T, C = (64, 192, 128)
        NH, NKV = (4, 2)
        HD = C // NH
        NREP = NH // NKV
        NE, TOPK = (8, 2)
        HID = int(8 / 3 * C)
        EPS_RMS = 1e-06

        def _rope_tables(t_len):
            inv_freq = 1.0 / 10000.0 ** (np.arange(0, HD, 2, dtype=np.float32) / HD)
            t = np.arange(t_len, dtype=np.float32)
            freqs = np.outer(t, inv_freq)
            emb = np.concatenate([freqs, freqs], axis=-1)
            return (jnp.asarray(np.cos(emb)), jnp.asarray(np.sin(emb)))

        def _rotate_half(x):
            h = x.shape[-1] // 2
            return jnp.concatenate([-x[..., h:], x[..., :h]], axis=-1)

        def _rmsnorm(v, w):
            return v * jax.lax.rsqrt(jnp.mean(v * v, axis=-1, keepdims=True) + EPS_RMS) * w
        Bx, Tx, Cx = x.shape
        h = _rmsnorm(x, ln1_w)
        q = (h @ wq.T).reshape(Bx, Tx, NH, HD).transpose(0, 2, 1, 3)
        k = (h @ wk.T).reshape(Bx, Tx, NKV, HD).transpose(0, 2, 1, 3)
        v = (h @ wv.T).reshape(Bx, Tx, NKV, HD).transpose(0, 2, 1, 3)
        cos, sin = _rope_tables(Tx)
        cos, sin = (cos[None, None], sin[None, None])
        q = q * cos + _rotate_half(q) * sin
        k = k * cos + _rotate_half(k) * sin
        k = jnp.repeat(k, NREP, axis=1)
        v = jnp.repeat(v, NREP, axis=1)
        scores = jnp.einsum('bhtd,bhsd->bhts', q, k) / jnp.sqrt(jnp.float32(HD))
        causal = jnp.tril(jnp.ones((Tx, Tx), dtype=bool))
        scores = jnp.where(causal[None, None], scores, jnp.float32(-1e+30))
        att = jax.nn.softmax(scores, axis=-1)
        y = jnp.einsum('bhts,bhsd->bhtd', att, v).transpose(0, 2, 1, 3).reshape(Bx, Tx, Cx)
        x = x + y @ wo.T
        flat = _rmsnorm(x, ln2_w).reshape(-1, Cx)
        probs = jax.nn.softmax(flat @ router_w.T, axis=-1)
        tp, ti = jax.lax.top_k(probs, TOPK)
        tp = tp / (jnp.sum(tp, axis=-1, keepdims=True) + 1e-09)
        weights = jnp.sum(tp[..., None] * jax.nn.one_hot(ti, NE, dtype=flat.dtype), axis=1)
        out = jnp.zeros_like(flat)
        for e in range(NE):
            hh = jax.nn.silu(flat @ w1[e].T) * (flat @ w3[e].T)
            out = out + weights[:, e:e + 1] * (hh @ w2[e].T)
        return x + out.reshape(Bx, Tx, Cx)
    x = x + _L0_gnn_ref(_layernorm(x, axis=-1), adj, L0_gnn_epsilon, L0_gnn_W1, L0_gnn_b1, L0_gnn_rms_weight, L0_gnn_W2, L0_gnn_b2)
    x = x + _L0_ffn_ref(_layernorm(x, axis=-1), L0_ffn_ln1_w, L0_ffn_ln2_w, L0_ffn_wq, L0_ffn_wk, L0_ffn_wv, L0_ffn_wo, L0_ffn_router_w, L0_ffn_w1, L0_ffn_w2, L0_ffn_w3)
    return x

_drawn_inputs = setup_inputs


def setup_inputs(seed=0):
    import zlib

    import numpy as np

    out = dict(_drawn_inputs(seed))
    spreads = {'L0_gnn_b1': (0.0, 0.1),
     'L0_gnn_rms_weight': (1.0, 0.2),
     'L0_gnn_b2': (0.0, 0.1),
     'L0_ffn_ln1_w': (1.0, 0.6),
     'L0_ffn_ln2_w': (1.0, 0.6)}
    factors = {'L0_ffn_wq': 8.0,
     'L0_ffn_wk': 8.0,
     'L0_ffn_wv': 6.983,
     'L0_ffn_wo': 6.708,
     'L0_ffn_router_w': 8.0,
     'L0_ffn_w1': 8.0,
     'L0_ffn_w2': 8.0,
     'L0_ffn_w3': 8.0}
    for name, (base, spread) in spreads.items():
        noise = np.random.default_rng([zlib.crc32(name.encode()), seed]).standard_normal(out[name].shape)
        drawn = base * np.exp(spread * noise) if base else spread * noise
        out[name] = jnp.asarray(drawn.astype(out[name].dtype))
    for name, factor in factors.items():
        out[name] = (out[name] * factor).astype(out[name].dtype)
    return out
```

```python
import numpy as np
import concourse.bass as bass
from concourse import mybir
from contextlib import ExitStack

F32 = mybir.dt.float32
BF16 = mybir.dt.bfloat16
ALU = mybir.AluOpType
ACT = mybir.ActivationFunctionType
X_AXIS = mybir.AxisListType.X

BATCHES, TOKENS, DIM = 128, 128, 128
PER_GROUP = 4
GROUPS = BATCHES // PER_GROUP
COLS = PER_GROUP * TOKENS
GNN_HID = 512
GNN_CHUNKS = GNN_HID // 128
HEADS, KV_HEADS, HEAD_DIM = 4, 2, 32
EXPERTS = 8
HID = 341
HID_CHUNKS = [(0, 128), (128, 128), (256, HID - 256)]
LN_EPS, RMS_EPS = 1e-5, 1e-6
MASKED = -1e30


def gnn_attention_moe(nc, t):
    ctx = ExitStack()
    with ctx:
        def sb(name, shape, dt=F32):
            return ctx.enter_context(nc.sbuf_tensor(name, shape, dt))

        def bank(name):
            return ctx.enter_context(nc.psum_tensor(name, [128, COLS], F32))

        def sem(name):
            return ctx.enter_context(nc.semaphore(name))

        ident = sb("ident_sb", [128, 128])
        ident_bf = sb("ident_bf_sb", [128, 128], BF16)
        ones = sb("ones_sb", [128, 128])
        mask_rows = sb("mask_rows_sb", [128, COLS], BF16)
        mask_cols = sb("mask_cols_sb", [128, COLS], BF16)
        pick = sb("pick_sb", [128, PER_GROUP, 128], BF16)
        cos = sb("cos_sb", [128, 128])
        sin = sb("sin_sb", [128, 128])
        w1g = sb("w1g", [128, GNN_HID])
        b1g = sb("b1g", [128, GNN_CHUNKS])
        rmsw = sb("rmsw", [128, GNN_CHUNKS])
        w2g = sb("w2g", [128, GNN_CHUNKS, DIM])
        b2g = sb("b2g", [128, DIM])
        eps_col = sb("eps_col", [128, 1])
        eps_ident = sb("eps_ident", [128, 128])
        norm1 = sb("norm1", [128, 1])
        norm2 = sb("norm2", [128, 1])
        wq = sb("wq", [128, HEADS, HEAD_DIM])
        wq_rot = sb("wq_rot", [128, HEADS, HEAD_DIM])
        wk2 = sb("wk2", [128, KV_HEADS, HEAD_DIM])
        wk = sb("wk", [128, HEADS, HEAD_DIM])
        wk_rot = sb("wk_rot", [128, HEADS, HEAD_DIM])
        wv = sb("wv", [128, KV_HEADS * HEAD_DIM])
        wo = sb("wo", [128, DIM])
        wr = sb("wr", [128, EXPERTS])
        w1e = sb("w1e", [128, EXPERTS, HID])
        w3e = sb("w3e", [128, EXPERTS, HID])
        w2e = sb("w2e", [128, EXPERTS, 3, DIM])
        minus_half = sb("minus_half", [128, 8])
        ln_eps = sb("ln_eps", [128, PER_GROUP])
        rank8 = sb("rank8", [128, EXPERTS])

        xs = sb("xs", [128, GROUPS, COLS])
        logits = sb("logits", [128, GROUPS * PER_GROUP, EXPERTS])

        x_in = sb("x_in", [128, PER_GROUP, DIM])
        adj_in = sb("adj_in", [128, PER_GROUP, 128])
        adj_eps = sb("adj_eps", [128, PER_GROUP, 128])
        stats1 = sb("stats1", [128, PER_GROUP, 6])
        mv1 = sb("mv1", [128, PER_GROUP, 2])
        var1 = sb("var1", [128, PER_GROUP])
        rstd1 = sb("rstd1", [128, PER_GROUP])
        ln1 = sb("ln1", [128, PER_GROUP, DIM])
        xb = sb("xb", [128, PER_GROUP, DIM])
        agg = sb("agg", [128, COLS])
        hid = sb("hid", [128, GNN_CHUNKS, COLS])
        sq = sb("sq", [128, GNN_CHUNKS, COLS])
        ms = sb("ms", [128, PER_GROUP])
        rrms = sb("rrms", [128, PER_GROUP])
        diag = sb("diag", [128, PER_GROUP, 128])
        stats2 = sb("stats2", [128, PER_GROUP, 6])
        mv2 = sb("mv2", [128, PER_GROUP, 2])
        var2 = sb("var2", [128, 2, PER_GROUP])
        rstd2 = sb("rstd2", [128, 2, PER_GROUP])
        ln2 = sb("ln2", [128, PER_GROUP, DIM])
        hn = sb("hn", [128, PER_GROUP, DIM])
        hnT = sb("hnT", [128, COLS])
        rope = sb("rope", [128, 4, COLS])
        qT = sb("qT", [128, COLS])
        kT = sb("kT", [128, COLS])
        v_ones = sb("v_ones", [128, PER_GROUP, KV_HEADS, HEAD_DIM + 1])
        neg_max = sb("neg_max", [128, HEADS, PER_GROUP])
        neg_max_parts = sb("neg_max_parts", [128, HEADS, HEAD_DIM // PER_GROUP, PER_GROUP], BF16)
        neg_maxT = sb("neg_maxT", [128, 128], BF16)
        probs = sb("probs", [128, HEADS, COLS])
        rsum = sb("rsum", [128, PER_GROUP, HEADS])
        y = sb("y", [128, PER_GROUP, DIM])
        yT = sb("yT", [128, COLS])
        x2 = sb("x2", [128, PER_GROUP, DIM])
        x2_sq = sb("x2_sq", [128, DIM])
        ss2 = sb("ss2", [128, PER_GROUP])
        ms2 = sb("ms2", [128, PER_GROUP])
        rrms2 = sb("rrms2", [128, PER_GROUP])
        flat = sb("flat", [128, PER_GROUP, DIM])
        flT = sb("flT", [128, COLS])
        act_g = sb("act_g", [128, 2, COLS])
        hh = sb("hh", [128, 3, COLS])
        acc = sb("acc", [128, PER_GROUP, DIM])
        NT = BATCHES
        sq_half, hid_half = sq[:].rearrange("p c n -> p (c n)"), hid[:].rearrange("p c n -> p (c n)")
        e_p, e_q = (sq_half[:, n * 1024:(n + 1) * 1024].rearrange("p (b e) -> p b e", e=EXPERTS) for n in range(2))
        one1, gate = (hid_half[:, n * 1024:(n + 1) * 1024].rearrange("p (b e) -> p b e", e=EXPERTS) for n in range(2))
        tokens_in = sb("tokens_in", [128, 2, COLS])
        red = sb("red", [128, 5, NT])

        pa = [bank(f"pa{i}") for i in range(3)]
        pb = [bank(f"pb{i}") for i in range(5)]

        consts_in = sem("consts_in")
        weights_in = sem("weights_in")
        prep = sem("prep")
        pool_prep = sem("pool_prep")
        x_loaded = sem("x_loaded")
        adj_loaded = sem("adj_loaded")
        adj_ready = sem("adj_ready")
        stats1_done = sem("stats1_done")
        mv1_done = sem("mv1_done")
        var1_done = sem("var1_done")
        rstd1_done = sem("rstd1_done")
        ln1_done = sem("ln1_done")
        xb_done = sem("xb_done")
        agg_psum = sem("agg_psum")
        agg_done = sem("agg_done")
        hid_psum = sem("hid_psum")
        hid_done = sem("hid_done")
        sq_done = sem("sq_done")
        ms_psum = sem("ms_psum")
        ms_done = sem("ms_done")
        rrms_done = sem("rrms_done")
        diag_done = sem("diag_done")
        bcast_psum = sem("bcast_psum")
        scaled_done = sem("scaled_done")
        silu_done = sem("silu_done")
        gnn_psum = sem("gnn_psum")
        x1_done = sem("x1_done")
        stats2_done = sem("stats2_done")
        mv2_done = sem("mv2_done")
        var2_done = sem("var2_done")
        rstd2_done = sem("rstd2_done")
        ln2_done = sem("ln2_done")
        hn_done = sem("hn_done")
        hnT_psum = sem("hnT_psum")
        hnT_done = sem("hnT_done")
        qk_psum = sem("qk_psum")
        v_psum = sem("v_psum")
        v_done = sem("v_done")
        rope_done = sem("rope_done")
        qk_done = sem("qk_done")
        s_psum = sem("s_psum")
        max_done = sem("max_done")
        max_hi = sem("max_hi")
        max_parts = sem("max_parts")
        maxT_psum = sem("maxT_psum")
        maxT_done = sem("maxT_done")
        st_psum = sem("st_psum")
        probs_done = sem("probs_done")
        y_psum = sem("y_psum")
        rsum_done = sem("rsum_done")
        y_done = sem("y_done")
        yT_psum = sem("yT_psum")
        yT_done = sem("yT_done")
        wo_psum = sem("wo_psum")
        x2_done = sem("x2_done")
        xs_done = sem("xs_done")
        ss2_done = sem("ss2_done")
        ms2_done = sem("ms2_done")
        rrms2_done = sem("rrms2_done")
        flat_done = sem("flat_done")
        flT_psum = sem("flT_psum")
        flT_done = sem("flT_done")
        flT_kept = sem("flT_kept")
        router_psum = sem("router_psum")
        logits_done = sem("logits_done")
        route = sem("route")
        route_exp_in = sem("route_exp_in")
        route_exp = sem("route_exp")
        gates_done = sem("gates_done")
        g_psum = sem("g_psum")
        g_done = sem("g_done")
        u_psum = sem("u_psum")
        hh_done = sem("hh_done")
        e_psum = sem("e_psum")
        e_used = sem("e_used")
        acc_step = sem("acc_step")
        stored = sem("stored")
        tokens_loaded = [sem(f"tokens_loaded{k}") for k in range(2)]

        NARROW = [(mask_rows[:], hid[:, 0, :]), (mask_cols[:], hid[:, 1, :]),
                  (pick[:].rearrange("p b s -> p (b s)"), hid[:, 2, :]), (ident_bf[:], ident[:])]
        CONSTS = [(ident, "ident"), (hid[:, 0:3, :], "narrow"), (cos, "cos"), (sin, "sin"), (rank8, "rank8")]
        WEIGHTS = [(w1g, "w1g"), (b1g, "b1g"), (rmsw, "rmsw"), (w2g, "w2g"), (b2g, "b2g"), (eps_col, "eps"),
                   (norm1, "norm1"), (norm2, "norm2"), (wq, "wq"), (wk2, "wk"), (wv, "wv"), (wo, "wo"), (wr, "wr"),
                   (w1e, "w1e"), (w3e, "w3e"), (w2e, "w2e")]

        block = ctx.enter_context(nc.Block())

        def interleaved(eng, steps):
            def run(a, b):
                for which, step in steps:
                    if which == "AB":
                        step(a, b)
                    if which == "A" and a is not None:
                        step(a)
                    if which == "B" and b is not None:
                        step(b)
            run(0, None)
            run(1, 0)
            with eng.Fori(2, GROUPS) as i:
                run(i, i - 1)
            run(None, GROUPS - 1)

        @block.sync
        def _(sp):
            for dst, name in CONSTS:
                sp.dma_start(dst[:, :] if name != "narrow" else dst, t[name]).then_inc(consts_in, 16)
            for dst, name in WEIGHTS:
                sp.dma_start(dst[:], t[name]).then_inc(weights_in, 16)

            def load(g):
                sp.wait_ge(ln1_done, g)
                sp.wait_ge(xb_done, g)
                sp.dma_start(x_in[:], t["x"][bass.ds(g, 1)].rearrange("g n b c -> n (g b) c")).then_inc(x_loaded, 16)
                sp.wait_ge(adj_ready, g)
                sp.dma_start(adj_in[:], t["adj"][bass.ds(g, 1)].rearrange("g m b n -> m (g b) n")).then_inc(adj_loaded, 16)

            def keep(b):
                sp.wait_ge(flT_done, b + 1)
                sp.dma_start(t["flatT"][bass.ds(b, 1)].rearrange("g c n -> c (g n)"), flT[:]).then_inc(flT_kept, 16)
            load(0)
            load(1)
            with sp.Fori(2, GROUPS) as g:
                load(g)
                keep(g - 2)
            keep(GROUPS - 2)
            keep(GROUPS - 1)
            with sp.Fori(0, GROUPS) as g:
                sp.wait_ge(acc_step, 8 * g + 8)
                sp.dma_start(t["out"][bass.ds(g, 1)].rearrange("g n b c -> n (g b) c"), acc[:]).then_inc(stored, 16)
            sp.wait_ge(stored, 16 * GROUPS)

        @block.gpsimd
        def _(pool):
            pool.memset(ones[:], 1.0).then_inc(pool_prep, 1)
            pool.memset(minus_half[:], -0.5).then_inc(pool_prep, 1)
            pool.memset(v_ones[:], 1.0).then_inc(pool_prep, 1)
            pool.memset(ln_eps[:], LN_EPS).then_inc(pool_prep, 1)
            pool.memset(neg_max_parts[:], 0.0).then_inc(pool_prep, 1)
            pool.wait_ge(weights_in, 16 * len(WEIGHTS))
            pool.wait_ge(pool_prep, 5)

            def rstd_1(a):
                pool.wait_ge(mv1_done, a + 1)
                pool.tensor_tensor(var1[:], mv1[:, :, 1], ln_eps[:], ALU.add).then_inc(var1_done, 1)
                pool.wait_ge(var1_done, a + 1)
                pool.wait_ge(ln1_done, a)
                pool.tensor_tensor(rstd1[:], var1[:], minus_half[:, 0:4], ALU.pow).then_inc(rstd1_done, 1)
                pool.wait_ge(x_loaded, 16 * a + 16)
                pool.wait_ge(x1_done, a)
                pool.tensor_tensor(xb[:], x_in[:], b2g[:].unsqueeze(1).to_broadcast([128, PER_GROUP, DIM]),
                                   ALU.add).then_inc(xb_done, 1)

            def squares(a):
                for c in range(GNN_CHUNKS):
                    pool.wait_ge(hid_done, 4 * a + c + 1)
                    pool.wait_ge(ms_psum, a)
                    pool.tensor_tensor(sq[:, c, :], hid[:, c, :], hid[:, c, :], ALU.mult).then_inc(sq_done, 1)

            def rrms_1(a):
                pool.wait_ge(ms_done, a + 1)
                pool.wait_ge(diag_done, a)
                pool.tensor_tensor(rrms[:], ms[:], minus_half[:, 0:4], ALU.pow).then_inc(rrms_done, 1)

            def rstd_2(b):
                pool.wait_ge(mv2_done, b + 1)
                pool.wait_ge(rstd2_done, b)
                pool.tensor_tensor(var2[:, 0, :], mv2[:, :, 1], ln_eps[:], ALU.add)
                pool.tensor_scalar(var2[:, 1, :], mv2[:, :, 1], 1.0 + RMS_EPS, RMS_EPS * LN_EPS, ALU.mult,
                                   ALU.add).then_inc(var2_done, 1)
                pool.wait_ge(var2_done, b + 1)
                pool.wait_ge(hn_done, b)
                pool.tensor_tensor(rstd2[:].rearrange("p a b -> p (a b)"), var2[:].rearrange("p a b -> p (a b)"),
                                   minus_half[:, 0:8], ALU.pow).then_inc(rstd2_done, 1)

            def rope_sums(b):
                for n, dst in enumerate((qT, kT)):
                    pool.wait_ge(rope_done, 4 * b + 2 * n + 2)
                    pool.wait_ge(st_psum, 4 * b)
                    pool.tensor_tensor(dst[:], rope[:, 2 * n, :], rope[:, 2 * n + 1, :], ALU.add).then_inc(qk_done, 1)

            def rrms_2(b):
                pool.wait_ge(x2_done, b + 1)
                row = xs[:, bass.ds(b, 1), :].rearrange("p g n -> p (g n)")
                pool.wait_ge(ss2_done, 4 * b + 4)
                pool.tensor_tensor(row, row, x2[:].rearrange("p b c -> p (b c)"), ALU.add).then_inc(xs_done, 1)
                pool.tensor_scalar(ms2[:], ss2[:], 1.0 / DIM, RMS_EPS, ALU.mult, ALU.add).then_inc(ms2_done, 1)
                pool.wait_ge(ms2_done, b + 1)
                pool.wait_ge(flat_done, b)
                pool.tensor_tensor(rrms2[:], ms2[:], minus_half[:, 0:4], ALU.pow).then_inc(rrms2_done, 1)

            interleaved(pool, [("A", rstd_1), ("B", rstd_2), ("B", rope_sums), ("A", squares), ("A", rrms_1),
                               ("B", rrms_2)])
            pool.wait_ge(flT_kept, 16 * GROUPS)

            def fetch(pair):
                for k in range(2):
                    pool.wait_ge(u_psum, 24 * (2 * pair))
                    pool.dma_start(tokens_in[:, k, :], t["flatT"][bass.ds(2 * pair + k, 1)]
                                   .rearrange("g c n -> c (g n)")).then_inc(tokens_loaded[k], 16)
            fetch(0)
            with pool.Fori(1, GROUPS // 2) as pair:
                fetch(pair)

        @block.scalar
        def _(act):
            act.wait_ge(weights_in, 16 * len(WEIGHTS))
            act.wait_ge(pool_prep, 5)

            def agg_out(a):
                act.wait_ge(agg_psum, a + 1)
                act.wait_ge(hid_psum, 4 * a)
                act.copy(agg[:], pa[1][:]).then_inc(agg_done, 1)

            def hid_out(a):
                for c in range(GNN_CHUNKS):
                    act.wait_ge(hid_psum, 4 * a + c + 1)
                    act.wait_ge(gnn_psum, a)
                    act.activation(hid[:, c, :], pa[c % 2][:], ACT.Identity, bias=b1g[:, c:c + 1]).then_inc(hid_done, 1)

            def silus(a):
                for c in range(GNN_CHUNKS):
                    act.wait_ge(scaled_done, 4 * a + c + 1)
                    act.activation(hid[:, c, :], hid[:, c, :], ACT.Silu, scale=rmsw[:, c:c + 1]).then_inc(silu_done, 1)

            def hnT_out(b):
                act.wait_ge(hnT_psum, b + 1)
                act.wait_ge(v_psum, b)
                act.copy(hnT[:], pb[0][:]).then_inc(hnT_done, 1)

            def v_out(b):
                act.wait_ge(v_psum, b + 1)
                act.wait_ge(y_psum, 2 * b)
                act.copy(v_ones[:, :, :, 0:HEAD_DIM],
                         pb[0][:, 0:256].rearrange("p (b g d) -> p b g d", b=4, g=2)).then_inc(v_done, 1)

            def maxT_out(b):
                act.wait_ge(maxT_psum, b + 1)
                act.wait_ge(st_psum, 4 * b)
                act.copy(neg_maxT[:], pb[0][:, 0:64].bitcast(BF16)).then_inc(maxT_done, 1)

            def exps(b):
                for h in range(HEADS):
                    act.wait_ge(st_psum, 4 * b + h + 1)
                    act.wait_ge(y_psum, 2 * b)
                    act.activation(probs[:, h, :], pb[1 + h][:], ACT.Exp, scale=HEAD_DIM ** -0.5).then_inc(probs_done, 1)

            def yT_out(b):
                act.wait_ge(yT_psum, b + 1)
                act.wait_ge(wo_psum, b)
                act.copy(yT[:], pb[2][:]).then_inc(yT_done, 1)

            def x2_squares(b):
                act.wait_ge(x2_done, b + 1)
                act.wait_ge(ms2_done, b)
                for n in range(PER_GROUP):
                    act.activation(x2_sq[:], x2[:, n, :], ACT.Square, accum_out=ss2[:, n:n + 1]).then_inc(ss2_done, 1)
                    act.wait_ge(ss2_done, 4 * b + n + 1)

            def flT_out(b):
                act.wait_ge(flT_psum, b + 1)
                act.wait_ge(router_psum, b)
                act.wait_ge(flT_kept, 16 * b)
                act.copy(flT[:], pb[4][:]).then_inc(flT_done, 1)

            def logits_out(b):
                act.wait_ge(router_psum, b + 1)
                act.copy(logits[:, bass.ds(4 * b, 4), :], pb[2][:, 0:32].rearrange("p (b e) -> p b e", b=4)
                         ).then_inc(logits_done, 1)

            interleaved(act, [("A", agg_out), ("B", hnT_out), ("A", hid_out), ("B", v_out), ("B", maxT_out), ("B", exps),
                              ("B", yT_out), ("A", silus), ("B", x2_squares), ("B", flT_out), ("B", logits_out)])

            act.wait_ge(route_exp_in, 1)
            act.activation(e_p, e_p, ACT.Exp).then_inc(route_exp, 1)

            per = EXPERTS * 3

            def gate_silus(g):
                for e in range(EXPERTS):
                    for c, (lo, m) in enumerate(HID_CHUNKS):
                        n = per * g + 3 * e + c
                        act.wait_ge(g_psum, n + 1)
                        if 3 * e + c >= 2:
                            act.wait_ge(hh_done, n - 1)
                        else:
                            act.wait_ge(hh_done, per * g)
                        act.activation(act_g[0:m, (3 * e + c) % 2, :], pa[(3 * e + c) % 2][0:m, :],
                                       ACT.Silu).then_inc(g_done, 1)
            gate_silus(0)
            with act.Fori(1, GROUPS) as g:
                gate_silus(g)

        @block.vector
        def _(dve):
            dve.wait_ge(weights_in, 16 * len(WEIGHTS))
            dve.wait_ge(consts_in, 16 * len(CONSTS))
            dve.wait_ge(pool_prep, 5)
            for narrow, wide_values in NARROW:
                dve.tensor_copy(narrow, wide_values)
            half = HEAD_DIM // 2
            dve.tensor_scalar(wq[:], wq[:], norm1[:, 0:1], None, ALU.mult)
            dve.tensor_scalar(wk2[:], wk2[:], norm1[:, 0:1], None, ALU.mult)
            dve.tensor_scalar(wv[:], wv[:], norm1[:, 0:1], None, ALU.mult)
            dve.tensor_scalar(wr[:], wr[:], norm2[:, 0:1], None, ALU.mult)
            dve.tensor_scalar(w1e[:], w1e[:], norm2[:, 0:1], None, ALU.mult)
            dve.tensor_scalar(w3e[:], w3e[:], norm2[:, 0:1], None, ALU.mult)
            dve.tensor_scalar(eps_ident[:], ident[:], eps_col[:, 0:1], None, ALU.mult).then_inc(prep, 1)
            dve.wait_ge(prep, 1)
            for g in range(KV_HEADS):
                dve.tensor_copy(wk[:, 2 * g:2 * g + 2, :], wk2[:, g:g + 1, :].to_broadcast([128, 2, HEAD_DIM]))
            dve.tensor_scalar(wq_rot[:, :, 0:half], wq[:, :, half:], -1.0, None, ALU.mult)
            dve.tensor_copy(wq_rot[:, :, half:], wq[:, :, 0:half]).then_inc(prep, 1)
            dve.wait_ge(prep, 2)
            dve.tensor_scalar(wk_rot[:, :, 0:half], wk[:, :, half:], -1.0, None, ALU.mult)
            dve.tensor_copy(wk_rot[:, :, half:], wk[:, :, 0:half]).then_inc(prep, 1)

            def per_batch(ap):
                return ap.unsqueeze(1).to_broadcast([128, PER_GROUP, 128])

            def stats(a, b):
                if a is not None:
                    dve.wait_ge(x_loaded, 16 * a + 16)
                    for n in range(PER_GROUP):
                        last = dve.bn_stats(stats1[:, n, :], x_in[:, n, :])
                    last.then_inc(stats1_done, 1)
                if b is not None:
                    dve.wait_ge(x1_done, b + 1)
                    for n in range(PER_GROUP):
                        last = dve.bn_stats(stats2[:, n, :], xs[:, bass.ds(b, 1), n * DIM:(n + 1) * DIM]
                                            .rearrange("p g n -> p (g n)"))
                    last.then_inc(stats2_done, 1)
                    dve.wait_ge(stats2_done, b + 1)
                    dve.wait_ge(var2_done, b)
                if a is not None:
                    dve.wait_ge(stats1_done, a + 1)
                    dve.wait_ge(var1_done, a)
                    dve.wait_ge(adj_loaded, 16 * a + 16)
                    dve.wait_ge(agg_psum, a)
                    dve.tensor_tensor(adj_eps[:], adj_in[:], per_batch(eps_ident[:]), ALU.add).then_inc(adj_ready, 1)
                    for n in range(PER_GROUP):
                        last = dve.bn_aggr(mv1[:, n, :], stats1[:, n, :])
                    last.then_inc(mv1_done, 1)
                if b is not None:
                    for n in range(PER_GROUP):
                        last = dve.bn_aggr(mv2[:, n, :], stats2[:, n, :])
                    last.then_inc(mv2_done, 1)

            def norm_1(a):
                dve.wait_ge(rstd1_done, a + 1)
                dve.wait_ge(agg_psum, a)
                for n in range(PER_GROUP):
                    last = dve.tensor_scalar(ln1[:, n, :], x_in[:, n, :], mv1[:, n, 0:1], rstd1[:, n:n + 1],
                                             ALU.subtract, ALU.mult)
                last.then_inc(ln1_done, 1)

            def ms_out(a):
                dve.wait_ge(ms_psum, a + 1)
                dve.tensor_scalar(ms[:], pa[2][:, 0:4], 1.0 / GNN_HID, RMS_EPS, ALU.mult, ALU.add).then_inc(ms_done, 1)

            def diags(a):
                dve.wait_ge(rrms_done, a + 1)
                for n in range(PER_GROUP):
                    last = dve.tensor_scalar(diag[:, n, :], ident[:], rrms[:, n:n + 1], None, ALU.mult)
                last.then_inc(diag_done, 1)

            def scale_hid(a):
                dve.wait_ge(bcast_psum, a + 1)
                dve.wait_ge(sq_done, 4 * a + 4)
                for c in range(GNN_CHUNKS):
                    dve.tensor_tensor(hid[:, c, :], hid[:, c, :], pa[2][:], ALU.mult).then_inc(scaled_done, 1)

            def x1_out(a):
                dve.wait_ge(gnn_psum, a + 1)
                dve.wait_ge(xb_done, a + 1)
                dve.tensor_tensor(xs[:, bass.ds(a, 1), :].rearrange("p g n -> p (g n)"), pa[0][:],
                                  xb[:].rearrange("p b c -> p (b c)"), ALU.add).then_inc(x1_done, 1)

            def norm_2(b):
                dve.wait_ge(rstd2_done, b + 1)
                dve.wait_ge(hnT_psum, b)
                for r, dst in ((1, hn), (0, ln2)):
                    for n in range(PER_GROUP):
                        last = dve.tensor_scalar(dst[:, n, :], xs[:, bass.ds(b, 1), n * DIM:(n + 1) * DIM]
                                                 .rearrange("p g n -> p (g n)"), mv2[:, n, 0:1],
                                                 rstd2[:, r, n:n + 1], ALU.subtract, ALU.mult)
                    last.then_inc(hn_done if r else ln2_done, 1)

            def rope_products(b):
                dve.wait_ge(qk_done, 2 * b)
                for n in range(4):
                    dve.wait_ge(qk_psum, 4 * b + n + 1)
                    table = (cos, sin)[n % 2]
                    dve.tensor_tensor(rope[:, n, :].rearrange("p (b t) -> p b t", b=4),
                                      pb[1 + n][:].rearrange("p (b t) -> p b t", b=4), per_batch(table[:]),
                                      ALU.mult).then_inc(rope_done, 1)

            def maxes(b):
                dve.wait_ge(max_parts, b)
                for h in range(HEADS):
                    dve.wait_ge(s_psum, b + 1)
                    dve.tensor_reduce(neg_max[:, h, :], pb[1 + h][:].rearrange("p (b s) -> p b s", b=4), X_AXIS,
                                      ALU.max, negate=True).then_inc(max_done, 1)
                dve.wait_ge(max_done, 4 * b + 4)
                dve.wait_ge(maxT_psum, b)
                dve.tensor_copy(neg_max_parts[:, :, 0, :], neg_max[:]).then_inc(max_hi, 1)
                dve.wait_ge(max_hi, b + 1)
                dve.tensor_tensor(neg_max_parts[:, :, 1, :], neg_max[:], neg_max_parts[:, :, 0, :],
                                  ALU.subtract).then_inc(max_parts, 1)

            def y_out(b):
                for n in range(2):
                    rows = pb[n][:, 0:264].rearrange("p (b h d) -> p b h d", b=2, h=HEADS)
                    dve.wait_ge(y_psum, 2 * b + n + 1)
                    dve.reciprocal(rsum[:, 2 * n:2 * n + 2, :], rows[:, :, :, HEAD_DIM]).then_inc(rsum_done, 1)
                    dve.wait_ge(rsum_done, 2 * b + n + 1)
                    dve.wait_ge(yT_psum, b)
                    dve.tensor_tensor(y[:, 2 * n:2 * n + 2, :].rearrange("p b (h d) -> p b h d", h=HEADS),
                                      rows[:, :, :, 0:HEAD_DIM],
                                      rsum[:, 2 * n:2 * n + 2, :].unsqueeze(3).to_broadcast([128, 2, HEADS, HEAD_DIM]),
                                      ALU.mult).then_inc(y_done, 1)

            def x2_out(b):
                dve.wait_ge(wo_psum, b + 1)
                dve.wait_ge(xs_done, b)
                dve.wait_ge(ln2_done, b + 1)
                dve.tensor_tensor(x2[:].rearrange("p b c -> p (b c)"), pb[3][:], ln2[:].rearrange("p b c -> p (b c)"),
                                  ALU.add).then_inc(x2_done, 1)

            def flat_out(b):
                dve.wait_ge(rrms2_done, b + 1)
                dve.wait_ge(flT_psum, b)
                for n in range(PER_GROUP):
                    last = dve.tensor_scalar(flat[:, n, :], x2[:, n, :], rrms2[:, n:n + 1], None, ALU.mult)
                last.then_inc(flat_done, 1)

            interleaved(dve, [("AB", stats), ("A", norm_1), ("B", norm_2), ("B", rope_products),
                              ("A", ms_out), ("B", maxes), ("A", diags), ("A", scale_hid), ("B", y_out), ("B", x2_out),
                              ("A", x1_out), ("B", flat_out)])

            steps = [0]

            def link(ins):
                steps[0] += 1
                ins.then_inc(route, 1)
                dve.wait_ge(route, steps[0])

            def wide(ap):
                return ap.unsqueeze(2).to_broadcast([128, NT, EXPERTS])

            def rank(ap=rank8):
                return ap[:].unsqueeze(1).to_broadcast([128, NT, EXPERTS])

            dve.wait_ge(logits_done, GROUPS)
            link(dve.tensor_reduce(red[:, 0, :], logits[:], X_AXIS, ALU.max))
            dve.tensor_tensor(e_p, logits[:], wide(red[:, 0, :]), ALU.subtract).then_inc(route_exp_in, 1)
            dve.wait_ge(route_exp, 1)
            link(dve.tensor_reduce(red[:, 0, :], e_p, X_AXIS, ALU.add))
            link(dve.tensor_reduce(red[:, 1, :], e_p, X_AXIS, ALU.max))
            link(dve.tensor_tensor(e_q, e_p, wide(red[:, 1, :]), ALU.is_equal))
            link(dve.tensor_tensor(e_q, e_q, rank(), ALU.mult))
            link(dve.tensor_reduce(red[:, 2, :], e_q, X_AXIS, ALU.max))
            link(dve.tensor_tensor(one1, rank(), wide(red[:, 2, :]), ALU.is_equal))
            link(dve.scalar_tensor_tensor(e_q, one1, -2.0, e_p, ALU.mult, ALU.add))
            link(dve.tensor_reduce(red[:, 3, :], e_q, X_AXIS, ALU.max))
            link(dve.tensor_tensor(e_q, e_q, wide(red[:, 3, :]), ALU.is_equal))
            link(dve.tensor_tensor(e_q, e_q, rank(), ALU.mult))
            link(dve.tensor_reduce(red[:, 2, :], e_q, X_AXIS, ALU.max))
            link(dve.tensor_tensor(e_q, rank(), wide(red[:, 2, :]), ALU.is_equal))
            link(dve.tensor_tensor(e_q, e_q, one1, ALU.add))
            link(dve.tensor_tensor(e_p, e_p, e_q, ALU.mult))
            link(dve.tensor_tensor(red[:, 4, :], red[:, 1, :], red[:, 3, :], ALU.add))
            link(dve.scalar_tensor_tensor(red[:, 4, :], red[:, 0, :], 1e-9, red[:, 4, :], ALU.mult, ALU.add))
            link(dve.reciprocal(red[:, 0, :], red[:, 4, :]))
            dve.tensor_tensor(gate, e_p, wide(red[:, 0, :]), ALU.mult).then_inc(gates_done, 1)
            dve.wait_ge(gates_done, 1)

            per = EXPERTS * 3

            def combine(g):
                for e in range(EXPERTS):
                    for c, (lo, m) in enumerate(HID_CHUNKS):
                        n = per * g + 3 * e + c
                        dve.wait_ge(g_done, n + 1)
                        dve.wait_ge(u_psum, n + 1)
                        dve.wait_ge(e_psum, 8 * g + e)
                        dve.tensor_tensor(hh[0:m, c, :], pb[(3 * e + c) % 2][0:m, :], act_g[0:m, (3 * e + c) % 2, :],
                                          ALU.mult).then_inc(hh_done, 1)
                    dve.wait_ge(e_psum, 8 * g + e + 1)
                    if e == 0:
                        dve.wait_ge(stored, 16 * g)
                    else:
                        dve.wait_ge(acc_step, 8 * g + e)
                    for n in range(PER_GROUP):
                        before = (xs[:, bass.ds(g, 1), n * DIM:(n + 1) * DIM].rearrange("p g n -> p (g n)")
                                  if e == 0 else acc[:, n, :])
                        last = dve.scalar_tensor_tensor(
                            acc[:, n, :], pb[2 + e % 2][:, n * DIM:(n + 1) * DIM],
                            gate[:, bass.ds(4 * g + n, 1), e], before, ALU.mult, ALU.add)
                    last.then_inc(acc_step, 1)
            combine(0)
            with dve.Fori(1, GROUPS) as g:
                combine(g)

        @block.tensor
        def _(pe):
            pe.wait_ge(weights_in, 16 * len(WEIGHTS))
            pe.wait_ge(consts_in, 16 * len(CONSTS))
            pe.wait_ge(pool_prep, 5)
            pe.wait_ge(prep, 3)

            def cols(n):
                return slice(n * 128, (n + 1) * 128)

            def aggregate(a):
                pe.wait_ge(ln1_done, a + 1)
                pe.wait_ge(adj_ready, a + 1)
                for n in range(PER_GROUP):
                    last = pe.matmul(pa[1][:, cols(n)], ln1[:, n, :], adj_eps[:, n, :], start=True, stop=True)
                last.then_inc(agg_psum, 1)

            def hidden(a):
                pe.wait_ge(agg_done, a + 1)
                pe.wait_ge(x1_done, a)
                for c in range(GNN_CHUNKS):
                    if c >= 2:
                        pe.wait_ge(hid_done, 4 * a + c - 1)
                    pe.matmul(pa[c % 2][:], w1g[:, cols(c)], agg[:], start=True, stop=True).then_inc(hid_psum, 1)

            def mean_square(a):
                pe.wait_ge(sq_done, 4 * a + 4)
                pe.wait_ge(scaled_done, 4 * a)
                for n in range(PER_GROUP):
                    for c in range(GNN_CHUNKS):
                        last = pe.matmul(pa[2][:, n:n + 1], sq[:, c, cols(n)], ones[:, 0:1],
                                         start=(c == 0), stop=(c == GNN_CHUNKS - 1))
                last.then_inc(ms_psum, 1)

            def spread(a):
                pe.wait_ge(diag_done, a + 1)
                pe.matmul(pa[2][:], ones[:], diag[:].rearrange("p b n -> p (b n)"), start=True,
                          stop=True).then_inc(bcast_psum, 1)

            def gnn_out(a):
                pe.wait_ge(silu_done, 4 * a + 4)
                for n in range(PER_GROUP):
                    for c in range(GNN_CHUNKS):
                        last = pe.matmul(pa[0][:, cols(n)], hid[:, c, cols(n)], w2g[:, c, :],
                                         start=(c == 0), stop=(c == GNN_CHUNKS - 1))
                last.then_inc(gnn_psum, 1)

            def hn_turn(b):
                pe.wait_ge(hn_done, b + 1)
                pe.wait_ge(y_done, 2 * b)
                for n in range(PER_GROUP):
                    last = pe.transpose(pb[0][:, cols(n)], hn[:, n, :], ident[:])
                last.then_inc(hnT_psum, 1)

            def qkv(b):
                pe.wait_ge(hnT_done, b + 1)
                pe.wait_ge(logits_done, b)
                pe.wait_ge(flT_done, b)
                pe.wait_ge(x2_done, b)
                for n, w in enumerate((wq, wq_rot, wk, wk_rot)):
                    pe.matmul(pb[1 + n][:], w[:].rearrange("p h d -> p (h d)"), hnT[:], start=True,
                              stop=True).then_inc(qk_psum, 1)
                for n in range(PER_GROUP):
                    last = pe.matmul(pb[0][:, 64 * n:64 * n + 64], hnT[:, cols(n)], wv[:], start=True, stop=True)
                last.then_inc(v_psum, 1)

            def scores(b):
                pe.wait_ge(qk_done, 2 * b + 2)
                for h in range(HEADS):
                    pe.matmul(pb[1 + h][:], ident_bf[:], mask_rows[:], start=True, stop=False)
                for n in range(PER_GROUP):
                    for h in range(HEADS):
                        part = slice(32 * h, 32 * h + 32)
                        last = pe.matmul(pb[1 + h][:, cols(n)], qT[part, cols(n)], kT[part, cols(n)], start=False,
                                         stop=(n == 3))
                last.then_inc(s_psum, 1)

            def max_turn(b):
                pe.wait_ge(max_parts, b + 1)
                pe.wait_ge(v_done, b + 1)
                pe.transpose(pb[0][:, 0:64].bitcast(BF16), neg_max_parts[:].rearrange("p h a b -> p (h a b)"),
                             ident_bf[:]).then_inc(maxT_psum, 1)

            def scoresT(b):
                for h in range(HEADS):
                    pe.wait_ge(max_done, 4 * b + h + 1)
                    pe.matmul(pb[1 + h][:], ident_bf[:], mask_cols[:], start=True, stop=False)
                for n in range(PER_GROUP):
                    for h in range(HEADS):
                        part = slice(32 * h, 32 * h + 32)
                        pe.matmul(pb[1 + h][:, cols(n)], kT[part, cols(n)], qT[part, cols(n)], start=False, stop=False)
                pe.wait_ge(maxT_done, b + 1)
                for n in range(PER_GROUP):
                    for h in range(HEADS):
                        part = slice(32 * h, 32 * h + 32)
                        last = pe.matmul(pb[1 + h][:, cols(n)], pick[part, n, :], neg_maxT[part, :], start=False,
                                         stop=(n == 3))
                        if n == 3:
                            last.then_inc(st_psum, 1)

            def attend(b):
                for n in range(PER_GROUP):
                    if n == 0:
                        pe.wait_ge(probs_done, 4 * b + 4)
                    for h in range(HEADS):
                        at = ((n % 2) * HEADS + h) * (HEAD_DIM + 1)
                        last = pe.matmul(pb[n // 2][:, at:at + HEAD_DIM + 1], probs[:, h, cols(n)],
                                         v_ones[:, n, h // 2, :], start=True, stop=True)
                    if n % 2:
                        last.then_inc(y_psum, 1)

            def y_turn(b):
                pe.wait_ge(y_done, 2 * b + 2)
                for n in range(PER_GROUP):
                    last = pe.transpose(pb[2][:, cols(n)], y[:, n, :], ident[:])
                last.then_inc(yT_psum, 1)

            def project(b):
                pe.wait_ge(yT_done, b + 1)
                for n in range(PER_GROUP):
                    last = pe.matmul(pb[3][:, cols(n)], yT[:, cols(n)], wo[:], start=True, stop=True)
                last.then_inc(wo_psum, 1)

            def flat_turn(b):
                pe.wait_ge(flat_done, b + 1)
                for n in range(PER_GROUP):
                    last = pe.transpose(pb[4][:, cols(n)], flat[:, n, :], ident[:])
                last.then_inc(flT_psum, 1)

            def router(b):
                pe.wait_ge(flT_done, b + 1)
                for n in range(PER_GROUP):
                    last = pe.matmul(pb[2][:, 8 * n:8 * n + 8], flT[:, cols(n)], wr[:], start=True, stop=True)
                last.then_inc(router_psum, 1)

            interleaved(pe, [("A", aggregate), ("B", hn_turn), ("A", hidden), ("B", qkv), ("B", scores),
                             ("A", mean_square), ("B", max_turn), ("B", scoresT), ("A", spread), ("B", attend),
                             ("B", y_turn), ("B", project), ("A", gnn_out), ("B", flat_turn), ("B", router)])

            per = EXPERTS * 3

            def group(g, tokens):
                def up(e, c):
                    lo, m = HID_CHUNKS[c]
                    k = 3 * e + c
                    n = per * g + k
                    if k >= 2:
                        pe.wait_ge(g_done, n - 1)
                        pe.wait_ge(hh_done, n - 1)
                    else:
                        pe.wait_ge(g_done, per * g)
                        pe.wait_ge(hh_done, per * g)
                    pe.matmul(pa[k % 2][0:m, :], w1e[:, e, lo:lo + m], tokens, start=True, stop=True).then_inc(g_psum, 1)
                    pe.matmul(pb[k % 2][0:m, :], w3e[:, e, lo:lo + m], tokens, start=True, stop=True).then_inc(u_psum, 1)

                def down(e):
                    pe.wait_ge(hh_done, per * g + 3 * e + 3)
                    if e >= 2:
                        pe.wait_ge(acc_step, 8 * g + e - 1)
                    else:
                        pe.wait_ge(acc_step, 8 * g)
                    for n in range(PER_GROUP):
                        for c, (lo, m) in enumerate(HID_CHUNKS):
                            last = pe.matmul(pb[2 + e % 2][:, cols(n)], hh[0:m, c, cols(n)], w2e[0:m, e, c, :],
                                             start=(c == 0), stop=(c == 2))
                    last.then_inc(e_psum, 1)

                for e in range(EXPERTS):
                    for c in range(3):
                        up(e, c)
                    down(e)

            def two_groups(pair):
                for k in range(2):
                    pe.wait_ge(tokens_loaded[k], 16 * pair + 16)
                    group(2 * pair + k, tokens_in[:, k, :])
            two_groups(0)
            with pe.Fori(1, GROUPS // 2) as pair:
                two_groups(pair)


def tables():
    inv_freq = 1.0 / 10000.0 ** (np.arange(0, HEAD_DIM, 2, dtype=np.float32) / HEAD_DIM)
    freqs = np.outer(np.arange(TOKENS, dtype=np.float32), inv_freq)
    emb = np.concatenate([freqs, freqs], axis=-1).astype(np.float32)
    later = np.arange(TOKENS)[None, :] > np.arange(TOKENS)[:, None]
    mask = np.where(later, MASKED, 0.0)
    pick = np.zeros((HEADS, HEAD_DIM, PER_GROUP, 128))
    for n in range(PER_GROUP):
        pick[:, n, n] = pick[:, PER_GROUP + n, n] = 1.0
    pick = pick.reshape(128, PER_GROUP, 128)
    return {
        "ident": np.eye(128, dtype=np.float32),
        "narrow": np.stack([np.tile(mask, (1, PER_GROUP)), np.tile(mask.T, (1, PER_GROUP)),
                            pick.reshape(128, COLS)], axis=1).astype(np.float32),
        "cos": np.tile(np.cos(emb).T, (HEADS, 1)).astype(np.float32),
        "sin": np.tile(np.sin(emb).T, (HEADS, 1)).astype(np.float32),
        "rank8": np.tile(np.arange(EXPERTS, 0, -1, dtype=np.float32), (128, 1)),
    }


def kernel(**inputs):
    import concourse.bacc as bacc
    from concourse.bass_utils import run_bass_kernel_spmd

    def arr(name):
        return np.asarray(inputs[name])

    def grouped(a):
        return a.reshape(GROUPS, PER_GROUP, 128, 128)

    w2 = np.zeros((128, EXPERTS, 3, DIM), np.float32)
    for c, (lo, m) in enumerate(HID_CHUNKS):
        w2[:m, :, c, :] = arr("L0_ffn_w2")[:, :, lo:lo + m].transpose(2, 0, 1)
    laid = {
        "x": grouped(arr("x")).transpose(0, 2, 1, 3),
        "adj": grouped(arr("adj")).transpose(0, 3, 1, 2),
        "w1g": arr("L0_gnn_W1"),
        "b1g": arr("L0_gnn_b1").reshape(GNN_CHUNKS, 128).T,
        "rmsw": arr("L0_gnn_rms_weight").reshape(GNN_CHUNKS, 128).T,
        "w2g": arr("L0_gnn_W2").reshape(GNN_CHUNKS, 128, DIM).transpose(1, 0, 2),
        "b2g": np.broadcast_to(arr("L0_gnn_b2"), (128, DIM)),
        "eps": np.broadcast_to(arr("L0_gnn_epsilon"), (128, 1)),
        "norm1": arr("L0_ffn_ln1_w").reshape(DIM, 1),
        "norm2": arr("L0_ffn_ln2_w").reshape(DIM, 1),
        "wq": arr("L0_ffn_wq").T.reshape(DIM, HEADS, HEAD_DIM),
        "wk": arr("L0_ffn_wk").T.reshape(DIM, KV_HEADS, HEAD_DIM),
        "wv": arr("L0_ffn_wv").T,
        "wo": arr("L0_ffn_wo").T,
        "wr": arr("L0_ffn_router_w").T,
        "w1e": arr("L0_ffn_w1").transpose(2, 0, 1),
        "w3e": arr("L0_ffn_w3").transpose(2, 0, 1),
        "w2e": w2,
    }
    laid.update(tables())

    nc = bacc.Bacc("TRN2", target_bir_lowering=False, num_devices=1)
    arrays, t = {}, {}
    for name, a in laid.items():
        a = np.ascontiguousarray(a)
        arrays[f"in_{name}"] = a
        t[name] = nc.dram_tensor(f"in_{name}", a.shape, mybir.dt.from_np(a.dtype), kind="ExternalInput").ap()
    t["out"] = nc.dram_tensor("out", (GROUPS, 128, PER_GROUP, DIM), F32, kind="ExternalOutput").ap()
    t["flatT"] = nc.dram_tensor("flatT", (GROUPS, 128, COLS), F32, kind="Internal").ap()
    gnn_attention_moe(nc, t)
    r = run_bass_kernel_spmd(nc, [arrays], core_ids=[0])
    out = r.results[0]["out"]
    return out.transpose(0, 2, 1, 3).reshape(BATCHES, TOKENS, DIM)
```

```python
import numpy as np
import concourse.bass as bass
from concourse import mybir
from contextlib import ExitStack

F32 = mybir.dt.float32
BF16 = mybir.dt.bfloat16
I32, U32 = mybir.dt.int32, mybir.dt.uint32
ALU = mybir.AluOpType
ACT = mybir.ActivationFunctionType
X_AXIS = mybir.AxisListType.X

BATCHES, TOKENS, DIM = 128, 128, 128
PER_GROUP = 4
GROUPS = BATCHES // PER_GROUP
COLS = PER_GROUP * TOKENS
GNN_HID = 512
GNN_CHUNKS = GNN_HID // 128
HEADS, KV_HEADS, HEAD_DIM = 4, 2, 32
HEAD_ORDER = [g * (HEADS // KV_HEADS) + n for n in range(HEADS // KV_HEADS) for g in range(KV_HEADS)]
EXPERTS = 8
HID = 341
HID_CHUNKS = [(0, 128), (128, 128), (256, HID - 256)]
LN_EPS, RMS_EPS = 1e-5, 1e-6
MASKED = -1e30
ALL_TOKENS = BATCHES * TOKENS
CHOICES = 2
LISTS = CHOICES * EXPERTS
LIST_ROWS = ALL_TOKENS + 128
TILES_PER_CHOICE = ALL_TOKENS // 128 + EXPERTS
TILES = CHOICES * TILES_PER_CHOICE
UNUSED = CHOICES * EXPERTS
PAD_ROW = LISTS * LIST_ROWS
SORTED_ROWS = PAD_ROW + UNUSED * 128
DUMPS = LISTS + UNUSED
ROW_GATES, ROW_TOKEN, ROW = DIM, DIM + CHOICES, DIM + 4
TABLE_COLS = -(-TILES_PER_CHOICE // 128)
UNROLL = 8
TURNS = TILES_PER_CHOICE // UNROLL


def gnn_attention_moe(nc, t):
    ctx = ExitStack()
    with ctx:
        def sb(name, shape, dt=F32):
            return ctx.enter_context(nc.sbuf_tensor(name, shape, dt))

        def bank(name):
            return ctx.enter_context(nc.psum_tensor(name, [128, COLS], F32))

        def sem(name):
            return ctx.enter_context(nc.semaphore(name))

        ident = sb("ident_sb", [128, 128])
        ident_bf = sb("ident_bf", [128, 128], BF16)
        ones = sb("ones", [128, 128])
        ones_bf = sb("ones_bf", [128, 128], BF16)
        before_bf = sb("before_bf", [128, 128], BF16)
        mask_rows = sb("mask_rows", [128, COLS], BF16)
        cos = sb("cos_sb", [128, 128])
        sin = sb("sin_sb", [128, 128])
        cos_sin = sb("cos_sin_sb", [128, 128])
        index8 = sb("index8", [128, EXPERTS])
        list_base = sb("list_base", [128, LISTS])
        tile_no = sb("tile_no", [128, CHOICES, TABLE_COLS])
        tile_first = sb("tile_first", [128, 1])
        choice_row = sb("choice_row", [128, CHOICES, TABLE_COLS])
        choice_pad = sb("choice_pad", [128, CHOICES, TABLE_COLS])
        w1g = sb("w1g", [128, GNN_HID])
        w1gT = sb("w1gT", [128, GNN_CHUNKS, DIM])
        b1g = sb("b1g", [128, GNN_CHUNKS])
        b1g_sq = sb("b1g_sq", [128, GNN_CHUNKS])
        rmsw = sb("rmsw", [128, GNN_CHUNKS])
        w2g = sb("w2g", [128, GNN_CHUNKS, DIM])
        b2g = sb("b2g", [128, DIM])
        gram = sb("gram", [128, DIM])
        gram_b = sb("gram_b", [128, 1])
        ms_base = sb("ms_base", [128, 1])
        ms_least = sb("ms_least", [128, 1])
        eps_col = sb("eps_col", [128, 1])
        eps_ident = sb("eps_ident", [128, 128])
        norm1 = sb("norm1", [128, 1])
        norm2 = sb("norm2", [128, 1])
        wq = sb("wq", [128, HEADS, HEAD_DIM])
        wq_rot = sb("wq_rot", [128, HEADS, HEAD_DIM])
        wk_alone = sb("wk_alone", [128, KV_HEADS, HEAD_DIM])
        wk = sb("wk", [128, 2, KV_HEADS, HEAD_DIM])
        wv = sb("wv", [128, KV_HEADS * HEAD_DIM])
        wo = sb("wo", [128, DIM])
        wr = sb("wr", [128, EXPERTS])
        w1e = sb("w1e", [128, EXPERTS, HID])
        w3e = sb("w3e", [128, EXPERTS, HID])
        w2e = sb("w2e", [128, EXPERTS, 3, DIM])
        minus_half = sb("minus_half", [128, PER_GROUP])
        plus_half = sb("plus_half", [128, PER_GROUP])
        ln_eps = sb("ln_eps", [128, PER_GROUP])
        rms_eps = sb("rms_eps", [128, PER_GROUP])
        held = sb("held", [128, 1])
        dim_inv = sb("dim_inv", [128, PER_GROUP])
        group_tokens = sb("group_tokens", [128, PER_GROUP])

        xs = sb("xs", [128, GROUPS, COLS])

        adj_in = sb("adj_in", [128, PER_GROUP, 128])
        adj_eps = sb("adj_eps", [128, PER_GROUP, 128])
        stats1 = sb("stats1", [128, PER_GROUP, 6])
        mv1 = sb("mv1", [128, PER_GROUP, 2])
        var1 = sb("var1", [128, PER_GROUP])
        rstd1 = sb("rstd1", [128, PER_GROUP])
        ln1 = sb("ln1", [128, PER_GROUP, DIM])
        agg = sb("agg", [128, COLS])
        agg_gram = sb("agg_gram", [128, COLS])
        ms_sum = sb("ms_sum", [128, PER_GROUP])
        ms = sb("ms", [128, PER_GROUP])
        rrms = sb("rrms", [128, PER_GROUP])
        rrms_wide = sb("rrms_wide", [128, PER_GROUP, 128])
        rrms_cols = sb("rrms_cols", [128, COLS])
        hid = sb("hid", [128, GNN_CHUNKS, COLS])
        stats2 = sb("stats2", [128, PER_GROUP, 6])
        carry = sb("carry", [128, 1])
        mv2 = sb("mv2", [128, PER_GROUP, 2])
        var2 = sb("var2", [128, 2, PER_GROUP])
        rstd2 = sb("rstd2", [128, PER_GROUP])
        ratio_parts = sb("ratio_parts", [128, 2, PER_GROUP])
        ratio2 = sb("ratio2", [128, PER_GROUP])
        ln2 = sb("ln2", [128, PER_GROUP, DIM])
        hn = sb("hn", [128, PER_GROUP, DIM])
        hnT = sb("hnT", [128, COLS])
        rope_k = sb("rope_k", [128, COLS])
        rope_q = sb("rope_q", [128, 2, COLS])
        qT = sb("qT", [128, COLS])
        kT = sb("kT", [128, COLS])
        v = sb("v", [128, PER_GROUP, KV_HEADS, HEAD_DIM])
        neg_max = sb("neg_max", [128, HEADS, PER_GROUP])
        probs = sb("probs", [128, HEADS, COLS])
        probsT = sb("probsT", [128, HEADS, COLS])
        prob_sums = sb("prob_sums", [128, PER_GROUP, HEADS])
        rsum = sb("rsum", [128, PER_GROUP, HEADS])
        rsum_wide = sb("rsum_wide", [128, PER_GROUP, HEADS, HEAD_DIM])
        rsumT = sb("rsumT", [128, COLS])
        yT = sb("yT", [128, COLS])
        x2 = sb("x2", [128, PER_GROUP, DIM])
        x2_sq = sb("x2_sq", [128, DIM])
        ss2 = sb("ss2", [128, PER_GROUP])
        ms2 = sb("ms2", [128, PER_GROUP])
        rrms2 = sb("rrms2", [128, PER_GROUP])
        rows = sb("rows", [128, PER_GROUP, ROW])
        flT = sb("flT", [128, COLS])
        logits = sb("logits", [128, PER_GROUP, EXPERTS])
        sorted8 = sb("sorted8", [128, PER_GROUP, EXPERTS])
        order8 = sb("order8", [128, PER_GROUP, EXPERTS], U32)
        order2 = sb("order2", [128, PER_GROUP, CHOICES])
        chosen = sb("chosen", [128, PER_GROUP, CHOICES, EXPERTS], BF16)
        under_max = sb("under_max", [128, PER_GROUP, EXPERTS])
        numer8 = sb("numer8", [128, PER_GROUP, EXPERTS])
        gate_sums = sb("gate_sums", [128, 3, PER_GROUP])
        list_end = sb("list_end", [128, LISTS])
        rank = sb("rank", [128, PER_GROUP, LISTS])
        slot_f = sb("slot_f", [128, PER_GROUP, CHOICES])
        slot = sb("slot", [128, PER_GROUP, CHOICES], I32)
        ends_i = sb("ends_i", [1, LISTS], I32)
        count_f = sb("count_f", [128, LISTS])
        over = sb("over", [128, LISTS])
        tiles_f = sb("tiles_f", [128, LISTS])
        first_tile = sb("first_tile", [128, CHOICES, EXPERTS + 1])
        past = sb("past", [128, CHOICES, TABLE_COLS, EXPERTS])
        expert_f = sb("expert_f", [128, CHOICES, TABLE_COLS])
        local_f = sb("local_f", [128, CHOICES, TABLE_COLS])
        unused_f = sb("unused_f", [128, CHOICES, TABLE_COLS])
        used_f = sb("used_f", [128, CHOICES, TABLE_COLS])
        table_cols = sb("table_cols", [128, 2, CHOICES, TABLE_COLS])
        table_diag = probs[:, 0:2, :]
        tile_row = sb("tile_row", [1, CHOICES * TILES_PER_CHOICE], I32)
        tile_expert = sb("tile_expert", [1, CHOICES * TILES_PER_CHOICE], I32)
        zero_rows = sb("zero_rows", [128, DIM])
        pad_tail = sb("pad_tail", [128, DUMPS, ROW - DIM])
        tile_in = sb("tile_in", [128, UNROLL, ROW])
        tokT = sb("tokT", [128, 2, 128])
        expert_space = probsT[:].rearrange("p h n -> p (h n)")
        act_g, hh = (expert_space[:, 2 * n * HID:2 * (n + 1) * HID].rearrange("p (u n) -> p u n", u=2)
                     for n in range(2))
        hhT = sb("hhT", [128, 2, 3, 128])
        expert_out = sb("expert_out", [128, UNROLL, DIM])
        token = sb("token", [128, UNROLL], I32)

        pa = [bank(f"pa{i}") for i in range(3)]
        pb = [bank(f"pb{i}") for i in range(5)]

        sems = {}

        def S(name):
            if name not in sems:
                sems[name] = sem(name)
            return sems[name]

        STAGED = [(mask_rows[:], hid[:, 0, :]), (ident_bf[:], ident[:]), (before_bf[:], hid[:, 1, 0:128]),
                  (ones_bf[:], ones[:])]
        CONSTS = [(ident[:], "ident"), (hid[:, 0:2, :], "narrow"), (cos[:], "cos"), (sin[:], "sin"),
                  (cos_sin[:], "cos_sin"), (index8[:], "index8"), (list_base[:], "list_base"),
                  (tile_no[:], "tile_no"), (tile_first[:], "tile_first"), (choice_row[:], "choice_row"),
                  (choice_pad[:], "choice_pad"), (pad_tail[:], "pad_tail"),
                  (rows[:, :, ROW_TOKEN:ROW], "first_tokens")]
        WEIGHTS = [(w1g[:], "w1g"), (w1gT[:], "w1gT"), (b1g[:], "b1g"), (rmsw[:], "rmsw"), (w2g[:], "w2g"),
                   (b2g[:], "b2g"), (eps_col[:], "eps"), (norm1[:], "norm1"), (norm2[:], "norm2"), (wq[:], "wq"),
                   (wk_alone[:], "wk"), (wv[:], "wv"), (wo[:], "wo"), (wr[:], "wr")]
        EXPERT_WEIGHTS = [(w1e[:], "w1e"), (w3e[:], "w3e"), (w2e[:], "w2e")]
        consts_in, weights_in, experts_in = sem("consts_in"), sem("weights_in"), sem("experts_in")
        scattered = [[sem(f"scattered{n}{k}") for k in range(CHOICES)] for n in range(PER_GROUP)]
        tile_loaded = [sem(f"tile_loaded{u}") for u in range(UNROLL)]
        added = [sem(f"added{u}") for u in range(UNROLL)]
        init_stored = [sem(f"init_stored{u}") for u in range(2)]

        block = ctx.enter_context(nc.Block())

        def pipelined(eng, steps, last_steps=None):
            lag = {"Z": 1, "A": 0, "B": -1, "C": -2, "D": -3}

            def turn(i, fixed, steps=steps):
                for stages, step in steps:
                    groups = {s: i + lag[s.upper()] for s in stages}
                    if fixed:
                        groups = {s: g if 0 <= g < GROUPS else None for s, g in groups.items()}
                    missing = [s for s, g in groups.items() if g is None]
                    if len(missing) < len(groups) and not any(s.isupper() for s in missing):
                        step(*groups.values())
            for i in range(-1, 4):
                turn(i, True)
            with eng.Fori(4, GROUPS - 1) as i:
                turn(i, False)
            turn(GROUPS - 1, True)
            for i in range(GROUPS, GROUPS + 3):
                turn(i, True, last_steps or steps)

        def tiles(eng, step, between=None):
            def turn(i):
                for u in range(UNROLL):
                    step(UNROLL * i + u, u)
            turn(0)
            with eng.Fori(1, TURNS) as i:
                turn(i)
            if between:
                between()
            turn(TURNS)
            with eng.Fori(TURNS + 1, 2 * TURNS - 1) as i:
                turn(i)
            turn(2 * TURNS - 1)

        def since(n, first):
            return not isinstance(n, int) or n >= first

        def x1_of(g, lo=0, hi=COLS):
            return xs[:, bass.ds(g, 1), lo:hi].rearrange("p g n -> p (g n)")

        def pad_rows(eng, first_row, n, tails, padded):
            body = t["sorted"][bass.ds(first_row, 128 * n)].rearrange("(n p) c -> p n c", p=128)
            eng.dma_start(body[:, :, 0:DIM], zero_rows[:].unsqueeze(1).to_broadcast([128, n, DIM])).then_inc(padded, 16)
            eng.dma_start(body[:, :, DIM:ROW], tails).then_inc(padded, 16)

        def pad_list(eng, n, padded):
            end = eng.value_load(ends_i[0:1, n:n + 1], min_val=n * LIST_ROWS, max_val=n * LIST_ROWS + ALL_TOKENS)
            pad_rows(eng, end, 1, pad_tail[:, n:n + 1, :], padded)

        @block.sync
        def _(sp):
            for dst, name in CONSTS:
                sp.dma_start(dst, t[name]).then_inc(consts_in, 16)
            for dst, name in WEIGHTS:
                sp.dma_start(dst, t[name]).then_inc(weights_in, 16)

            def load(z):
                sp.wait_ge(S("adj_ready"), z)
                sp.dma_start(xs[:, bass.ds(z, 1), :].rearrange("p g (b c) -> p (g b) c", b=PER_GROUP),
                             t["x"][bass.ds(z, 1)].rearrange("g n b c -> n (g b) c")).then_inc(S("x_loaded"), 16)
                sp.dma_start(adj_in[:], t["adj"][bass.ds(z, 1)].rearrange("g m b n -> m (g b) n")
                             ).then_inc(S("adj_loaded"), 16)

            def store_sums(c):
                sp.wait_ge(S("xs_done"), c + 1)
                sp.dma_start(t["out"][bass.ds(c * COLS, COLS)].rearrange("(b n) c -> n b c", b=PER_GROUP),
                             x1_of(c).rearrange("p (b c) -> p b c", b=PER_GROUP)).then_inc(S("sums_stored"), 16)

            load(0)
            for dst, name in EXPERT_WEIGHTS:
                sp.dma_start(dst, t[name]).then_inc(experts_in, 16)
            sp.wait_ge(S("pool_prep"), 1)
            sp.dma_start(t["out"][ALL_TOKENS:ALL_TOKENS + 128 * DUMPS].rearrange("(n p) c -> p n c", p=128),
                         zero_rows[:].unsqueeze(1).to_broadcast([128, DUMPS, DIM])).then_inc(S("sums_stored"), 16)
            for z in range(1, 4):
                load(z)
            with sp.Fori(4, GROUPS) as z:
                load(z)
                store_sums(z - 4)
            for c in range(GROUPS - 4, GROUPS):
                store_sums(c)

            sp.wait_ge(S("ends_done"), 1)
            pad_rows(sp, PAD_ROW, UNUSED, pad_tail[:, LISTS:DUMPS, :], S("padded_1"))
            for n in range(EXPERTS // 2):
                pad_list(sp, n, S("padded_1"))
            sp.wait_ge(S("padded_1"), 32 * (EXPERTS + 1))
            for n in range(PER_GROUP):
                for k in range(CHOICES):
                    sp.wait_ge(scattered[n][k], 16 * GROUPS)
            sp.wait_ge(S("tables_done"), CHOICES)

            def second_pads():
                sp.wait_ge(S("padded_2"), 32 * EXPERTS)

            def load_tile(n, u):
                row = sp.value_load(tile_row[0:1, bass.ds(n, 1)], min_val=0, max_val=SORTED_ROWS - 128)
                if since(n, UNROLL):
                    sp.wait_ge(S("scaled"), n - UNROLL + 1)
                    sp.wait_ge(S("token_done"), n - UNROLL + 1)
                sp.dma_start(tile_in[:, u, :], t["sorted"][bass.ds(row, 128)]).then_inc(tile_loaded[u], 16)
            tiles(sp, load_tile, second_pads)

        @block.gpsimd
        def _(pool):
            pool.memset(ones[:], 1.0)
            pool.memset(minus_half[:], -0.5)
            pool.memset(plus_half[:], 0.5)
            pool.memset(ln_eps[:], LN_EPS)
            pool.memset(rms_eps[:], RMS_EPS)
            pool.memset(dim_inv[:], 1.0 / DIM)
            pool.memset(group_tokens[:], float(COLS))
            pool.memset(zero_rows[:], 0.0).then_inc(S("pool_prep"), 1)
            pool.wait_ge(S("pool_prep"), 1)
            pool.wait_ge(weights_in, 16 * len(WEIGHTS))
            pool.wait_ge(consts_in, 16 * len(CONSTS))
            pool.wait_ge(S("prep"), 1)

            def add_epsilon(z):
                pool.wait_ge(S("adj_loaded"), 16 * z + 16)
                pool.wait_ge(S("agg_psum"), z)
                pool.tensor_tensor(adj_eps[:], adj_in[:], eps_ident[:].unsqueeze(1).to_broadcast([128, PER_GROUP, 128]),
                                   ALU.add).then_inc(S("adj_ready"), 1)

            def sums_out(d):
                pool.wait_ge(S("x2_done"), d + 1)
                pool.tensor_tensor(x1_of(d), x1_of(d), x2[:].rearrange("p b c -> p (b c)"), ALU.add
                                   ).then_inc(S("xs_done"), 1)

            def rstd_1(z):
                pool.wait_ge(S("mv1_done"), z + 1)
                pool.tensor_tensor(var1[:], mv1[:, :, 1], ln_eps[:], ALU.add).then_inc(S("var1_done"), 1)
                pool.wait_ge(S("var1_done"), z + 1)
                pool.wait_ge(S("ln1_done"), z)
                pool.tensor_tensor(rstd1[:], var1[:], minus_half[:, 0:4], ALU.pow).then_inc(S("rstd1_done"), 1)

            def add_b2(a):
                pool.wait_ge(S("ln1_done"), a + 1)
                x1 = x1_of(a).rearrange("p (b c) -> p b c", b=PER_GROUP)
                pool.tensor_tensor(x1, x1, b2g[:].unsqueeze(1).to_broadcast([128, PER_GROUP, DIM]),
                                   ALU.add).then_inc(S("b2_done"), 1)

            def rrms_1(a):
                pool.wait_ge(S("ms_done"), a + 1)
                pool.wait_ge(S("rrms_wide_done"), a)
                pool.tensor_tensor(rrms[:], ms[:], minus_half[:, 0:4], ALU.pow).then_inc(S("rrms_done"), 1)

            def tokens_step(d):
                if isinstance(d, int) and d == 0:
                    return
                for n in range(PER_GROUP):
                    for k in range(CHOICES):
                        pool.wait_ge(scattered[n][k], 16 * d)
                pool.tensor_tensor(rows[:, :, ROW_TOKEN], rows[:, :, ROW_TOKEN], group_tokens[:], ALU.add
                                   ).then_inc(S("rows_free"), 1)

            def rstd_2(b):
                pool.wait_ge(S("var2_done"), b + 1)
                pool.wait_ge(S("hn_done"), b)
                pool.tensor_tensor(rstd2[:], var2[:, 1, :], minus_half[:], ALU.pow).then_inc(S("rstd2_done"), 1)

            def ratio_2(b):
                pool.wait_ge(S("ln_var2_done"), b + 1)
                pool.tensor_tensor(ratio_parts[:, 0, :], var2[:, 0, :], minus_half[:], ALU.pow)
                pool.tensor_tensor(ratio_parts[:, 1, :], var2[:, 1, :], plus_half[:], ALU.pow
                                   ).then_inc(S("ratio_parts_done"), 1)
                pool.wait_ge(S("ratio_parts_done"), b + 1)
                pool.wait_ge(S("ln2_done"), b)
                pool.tensor_tensor(ratio2[:], ratio_parts[:, 0, :], ratio_parts[:, 1, :], ALU.mult
                                   ).then_inc(S("ratio2_done"), 1)

            def rrms_2(c):
                pool.wait_ge(S("ss2_done"), 4 * c + 4)
                pool.tensor_tensor(ms2[:], ss2[:], dim_inv[:], ALU.mult).then_inc(S("ms2_scaled"), 1)
                pool.wait_ge(S("ms2_scaled"), c + 1)
                pool.tensor_tensor(ms2[:], ms2[:], rms_eps[:], ALU.add).then_inc(S("ms2_done"), 1)
                pool.wait_ge(S("ms2_done"), c + 1)
                pool.wait_ge(S("flat_done"), c)
                pool.tensor_tensor(rrms2[:], ms2[:], minus_half[:, 0:4], ALU.pow).then_inc(S("rrms2_done"), 1)

            def hold(before):
                pool.wait_ge(S("held_done"), before)
                pool.tensor_tensor(held[:], ln_eps[:, 0:1], rms_eps[:, 0:1], ALU.add).then_inc(S("held_done"), 1)

            def scatter(d):
                pool.wait_ge(S("slot_done"), d + 1)
                pool.wait_ge(S("gates_done"), d + 1)
                pool.wait_ge(S("flat_done"), d + 1)
                hold(d)
                for n in range(PER_GROUP):
                    for k in range(CHOICES):
                        pool.indirect_dma_start(t["sorted"][:],
                                                bass.IndirectOffsetOnAxis(ap=slot[:, n, k:k + 1], axis=0),
                                                rows[:, n, :], None).then_inc(scattered[n][k], 16)

            pipelined(pool, [("D", tokens_step), ("B", rstd_2), ("D", sums_out), ("A", rrms_1), ("Z", rstd_1),
                             ("B", ratio_2), ("A", add_b2), ("Z", add_epsilon), ("D", scatter), ("C", rrms_2)],
                      [("D", tokens_step), ("B", rstd_2), ("D", sums_out), ("B", ratio_2), ("C", rrms_2),
                       ("D", scatter)])

            pool.wait_ge(S("ends_done"), 1)
            for n in range(EXPERTS, LISTS):
                pad_list(pool, n, S("padded_2"))

            pool.wait_ge(S("sums_stored"), 16 * GROUPS + 16)

            def add_tile(n, u):
                pool.wait_ge(S("scaled"), n + 1)
                pool.wait_ge(S("token_done"), n + 1)
                hold(GROUPS + n)
                pool.indirect_dma_start(t["out"][:], bass.IndirectOffsetOnAxis(ap=token[:, u:u + 1], axis=0),
                                        expert_out[:, u, :], None, compute_op=ALU.add).then_inc(added[u], 16)

            def all_added():
                for u in range(UNROLL):
                    pool.wait_ge(added[u], 16 * TURNS)
            tiles(pool, add_tile, all_added)
            for u in range(UNROLL):
                pool.wait_ge(added[u], 32 * TURNS)

        @block.scalar
        def _(act):
            act.wait_ge(weights_in, 16 * len(WEIGHTS))
            act.wait_ge(consts_in, 16 * len(CONSTS))
            act.wait_ge(S("pool_prep"), 1)

            def agg_out(a):
                act.wait_ge(S("agg_psum"), a + 1)
                act.wait_ge(S("hid_psum"), 4 * a)
                act.copy(agg[:], pa[2][:]).then_inc(S("agg_done"), 1)

            def rrms_widen(a):
                act.wait_ge(S("rrms_done"), a + 1)
                act.wait_ge(S("rrms_psum"), a)
                act.copy(rrms_wide[:], rrms[:].unsqueeze(2).to_broadcast([128, PER_GROUP, 128])
                         ).then_inc(S("rrms_wide_done"), 1)

            def rrms_out(a):
                act.wait_ge(S("rrms_psum"), a + 1)
                act.wait_ge(S("scaled_done"), 4 * a)
                act.copy(rrms_cols[:], pa[2][:]).then_inc(S("rrms_cols_done"), 1)

            def silus(a):
                for c in range(GNN_CHUNKS):
                    act.wait_ge(S("scaled_done"), 4 * a + c + 1)
                    act.activation(hid[:, c, :], hid[:, c, :], ACT.Silu, scale=rmsw[:, c:c + 1]
                                   ).then_inc(S("silu_done"), 1)

            def hnT_out(b):
                act.wait_ge(S("hnT_psum"), b + 1)
                act.wait_ge(S("v_psum"), b)
                act.copy(hnT[:], pb[1][:]).then_inc(S("hnT_done"), 1)

            def v_out(b):
                act.wait_ge(S("v_psum"), b + 1)
                act.wait_ge(S("y_psum"), b)
                act.copy(v[:], pb[0][:, 0:256].rearrange("p (b g d) -> p b g d", b=4, g=2)).then_inc(S("v_done"), 1)

            def exps(c, heads):
                for h in heads:
                    act.wait_ge(S("max_done"), 4 * c + h + 1)
                    act.wait_ge(S("pT_psum"), 4 * c)
                    act.wait_ge(S("rsum_done"), c)
                    for n in range(PER_GROUP):
                        last = act.activation(probs[:, h, n * 128:(n + 1) * 128], pb[1 + h][:, n * 128:(n + 1) * 128],
                                              ACT.Exp, bias=neg_max[:, h, n:n + 1],
                                              accum_out=prob_sums[:, n, h:h + 1])
                    last.then_inc(S("probs_done"), 1)

            def exps_1(c):
                exps(c, range(3))

            def exps_2(c):
                exps(c, range(3, HEADS))

            def probsT_out(c):
                act.wait_ge(S("pT_psum"), 4 * c + 4)
                act.wait_ge(S("y_psum"), c)
                act.copy(probsT[:, HEADS - 1, :], pb[HEADS][:]).then_inc(S("pT_last_done"), 1)

            def ln2_out(b):
                act.wait_ge(S("ratio2_done"), b + 1)
                act.wait_ge(S("hn_done"), b + 1)
                act.wait_ge(S("x2_done"), b)
                for n in range(PER_GROUP):
                    last = act.activation(ln2[:, n, :], hn[:, n, :], ACT.Copy, scale=ratio2[:, n:n + 1])
                last.then_inc(S("ln2_done"), 1)

            def rsumT_out(c):
                act.wait_ge(S("rsumT_psum"), c + 1)
                act.wait_ge(S("yT_done"), c)
                act.copy(rsumT[:], pa[0][:]).then_inc(S("rsumT_done"), 1)

            def x2_squares(c):
                act.wait_ge(S("x2_done"), c + 1)
                act.wait_ge(S("ms2_done"), c)
                for n in range(PER_GROUP):
                    act.wait_ge(S("ss2_done"), 4 * c + n)
                    act.activation(x2_sq[:], x2[:, n, :], ACT.Square, accum_out=ss2[:, n:n + 1]
                                   ).then_inc(S("ss2_done"), 1)

            def flat_out(d):
                act.wait_ge(S("rrms2_done"), d + 1)
                act.wait_ge(S("rows_free"), d)
                act.wait_ge(S("flT_psum"), d)
                for n in range(PER_GROUP):
                    last = act.activation(rows[:, n, 0:DIM], x2[:, n, :], ACT.Copy, scale=rrms2[:, n:n + 1])
                last.then_inc(S("flat_done"), 1)

            def flT_out(d):
                act.wait_ge(S("flT_psum"), d + 1)
                act.wait_ge(S("router_psum"), d)
                act.copy(flT[:], pb[3][:]).then_inc(S("flT_done"), 1)

            def logits_out(d):
                act.wait_ge(S("router_psum"), d + 1)
                act.wait_ge(S("order_done"), 4 * d)
                act.copy(logits[:], pa[2][:, 0:32].rearrange("p (b e) -> p b e", b=4)).then_inc(S("logits_done"), 1)

            def numerators(d):
                act.wait_ge(S("under_max_done"), d + 1)
                act.wait_ge(S("gates_done"), d)
                act.activation(numer8[:], under_max[:], ACT.Exp).then_inc(S("numer_done"), 1)

            pipelined(act, [("C", exps_1), ("A", agg_out), ("C", exps_2), ("C", probsT_out), ("B", hnT_out),
                            ("D", flat_out), ("C", rsumT_out), ("D", flT_out), ("A", rrms_widen), ("D", logits_out),
                            ("D", numerators), ("B", v_out), ("A", rrms_out), ("C", x2_squares), ("B", ln2_out),
                            ("A", silus)])

            act.wait_ge(S("ends_done"), 1)
            for n in range(EXPERTS // 2, EXPERTS):
                pad_list(act, n, S("padded_1"))
            act.wait_ge(experts_in, 16 * len(EXPERT_WEIGHTS))
            act.activation(w1e[:], w1e[:], ACT.Copy, scale=norm2[:, 0:1])
            act.activation(w3e[:], w3e[:], ACT.Copy, scale=norm2[:, 0:1]).then_inc(S("experts_scaled"), 1)

            def columns(n, u):
                act.wait_ge(S("tokT_psum"), n + 1)
                if since(n, 2):
                    act.wait_ge(S("u_psum"), n - 1)
                act.copy(tokT[:, u % 2, :], pa[0][:, 0:128]).then_inc(S("tokT_done"), 1)

            def hidden_columns(n, u):
                act.wait_ge(S("hhT_psum"), n + 1)
                if since(n, 2):
                    act.wait_ge(S("e_psum"), n - 1)
                for c, (lo, m) in enumerate(HID_CHUNKS):
                    if c != 1:
                        parts = slice(0, 2) if c == 0 else slice(2, 3)
                        last = act.copy(hhT[0:m, u % 2, parts, :],
                                        pa[1][0:m, 128 * parts.start:128 * parts.stop].rearrange(
                                            "p (c n) -> p c n", n=128))
                last.then_inc(S("hhT_done"), 1)

            def expert(n, u):
                act.wait_ge(S("g_psum"), n + 1)
                if since(n, 2):
                    act.wait_ge(S("hh_done"), n - 1)
                act.activation(act_g[:, u % 2, :], pb[u % 2][:, 0:HID], ACT.Silu).then_inc(S("g_done"), 1)
                if not (isinstance(n, int) and n == TILES - 1):
                    columns(n + 1, u + 1)
                if since(n, 1):
                    hidden_columns(n - 1, u + 1)
            columns(0, 0)
            tiles(act, expert)
            hidden_columns(TILES - 1, 1)

        @block.vector
        def _(dve):
            dve.wait_ge(weights_in, 16 * len(WEIGHTS))
            dve.wait_ge(consts_in, 16 * len(CONSTS))
            dve.wait_ge(S("pool_prep"), 1)
            half = HEAD_DIM // 2
            for narrow, wide_values in STAGED:
                dve.tensor_copy(narrow, wide_values)
            dve.tensor_copy(list_end[:], list_base[:])
            dve.tensor_tensor(b1g_sq[:], b1g[:], b1g[:], ALU.mult)
            dve.tensor_scalar(wq[:], wq[:], norm1[:, 0:1], HEAD_DIM ** -0.5, ALU.mult, ALU.mult)
            dve.tensor_scalar(wk_alone[:], wk_alone[:], norm1[:, 0:1], None, ALU.mult)
            dve.tensor_scalar(wv[:], wv[:], norm1[:, 0:1], None, ALU.mult)
            dve.tensor_scalar(wr[:], wr[:], norm2[:, 0:1], None, ALU.mult)
            dve.tensor_scalar(eps_ident[:], ident[:], eps_col[:, 0:1], None, ALU.mult).then_inc(S("prep"), 1)
            dve.wait_ge(S("prep"), 1)
            dve.tensor_copy(wk[:, 0, :, :], wk_alone[:])
            dve.tensor_scalar(wk[:, 1, :, 0:half], wk_alone[:, :, half:], -1.0, None, ALU.mult)
            dve.tensor_copy(wk[:, 1, :, half:], wk_alone[:, :, 0:half])
            dve.tensor_scalar(wq_rot[:, :, 0:half], wq[:, :, half:], -1.0, None, ALU.mult)
            dve.tensor_copy(wq_rot[:, :, half:], wq[:, :, 0:half]).then_inc(S("prep"), 1)
            dve.wait_ge(S("gram_psum"), 1)
            dve.tensor_scalar(gram[:], pa[0][:, 0:128], 1.0 / GNN_HID, None, ALU.mult)
            dve.tensor_scalar(gram_b[:], pa[1][:, 0:1], 2.0 / GNN_HID, None, ALU.mult)
            dve.tensor_reduce(ms_base[:], pa[2][:, 0:4], X_AXIS, ALU.add).then_inc(S("prep"), 1)
            dve.wait_ge(S("prep"), 3)
            dve.tensor_scalar(ms_least[:], ms_base[:], -1.0 / GNN_HID, None, ALU.mult)
            dve.tensor_scalar(ms_base[:], ms_base[:], 1.0 / GNN_HID, RMS_EPS, ALU.mult, ALU.add).then_inc(S("prep"), 1)

            def per_batch(ap):
                return ap.unsqueeze(1).to_broadcast([128, PER_GROUP, 128])

            def stats_1(z):
                dve.wait_ge(S("x_loaded"), 16 * z + 16)
                for n in range(PER_GROUP):
                    last = dve.bn_stats(stats1[:, n, :], x1_of(z, n * DIM, (n + 1) * DIM))
                last.then_inc(S("stats1_done"), 1)
                dve.wait_ge(S("stats1_done"), z + 1)
                dve.wait_ge(S("var1_done"), z)
                dve.tensor_copy(carry[:], stats1[:, 0, 0:1])
                for n in range(PER_GROUP):
                    last = dve.bn_aggr(mv1[:, n, :], stats1[:, n, :])
                last.then_inc(S("mv1_done"), 1)

            def norm_1(z):
                dve.wait_ge(S("rstd1_done"), z + 1)
                dve.wait_ge(S("agg_psum"), z)
                for n in range(PER_GROUP):
                    last = dve.tensor_scalar(ln1[:, n, :], x1_of(z, n * DIM, (n + 1) * DIM), mv1[:, n, 0:1],
                                             rstd1[:, n:n + 1], ALU.subtract, ALU.mult)
                last.then_inc(S("ln1_done"), 1)

            def gram_product(a):
                dve.wait_ge(S("gram_agg_psum"), a + 1)
                dve.wait_ge(S("ms_psum"), a)
                dve.scalar_tensor_tensor(agg_gram[:], pa[0][:], gram_b[:, 0:1], agg[:], ALU.add, ALU.mult
                                         ).then_inc(S("gram_product_done"), 1)

            def ms_out(a):
                dve.wait_ge(S("ms_psum"), a + 1)
                dve.wait_ge(S("ms_done"), a)
                dve.tensor_reduce(ms_sum[:], pa[2][:].rearrange("p (b c) -> p b c", b=PER_GROUP), X_AXIS, ALU.add
                                  ).then_inc(S("ms_sum_done"), 1)
                dve.wait_ge(S("ms_sum_done"), a + 1)
                dve.tensor_scalar(ms[:], ms_sum[:], ms_least[:, 0:1], ms_base[:, 0:1], ALU.max, ALU.add
                                  ).then_inc(S("ms_done"), 1)

            def scale_hid(a, lo, hi):
                dve.wait_ge(S("rrms_cols_done"), a + 1)
                for c in range(lo, hi):
                    dve.wait_ge(S("hid_psum"), 4 * a + c + 1)
                    if c == 0:
                        dve.wait_ge(S("gnn_psum"), 2 * a)
                    dve.scalar_tensor_tensor(hid[:, c, :], pa[c % 2][:], b1g[:, c:c + 1], rrms_cols[:],
                                             ALU.add, ALU.mult).then_inc(S("scaled_done"), 1)

            def scale_hid_1(a):
                scale_hid(a, 0, 2)

            def scale_hid_2(a):
                scale_hid(a, 2, 4)

            def x1_out(a):
                dve.wait_ge(S("b2_done"), a + 1)
                for half in range(2):
                    x1 = x1_of(a, half * COLS // 2, (half + 1) * COLS // 2)
                    dve.wait_ge(S("gnn_psum"), 2 * a + half + 1)
                    dve.tensor_tensor(x1, pa[half][:, 0:COLS // 2], x1, ALU.add).then_inc(S("x1_done"), 1)
                    dve.wait_ge(S("x1_done"), 2 * a + half + 1)
                    dve.tensor_copy(carry[:], ln_eps[:, 0:1])
                    for n in range(2 * half, 2 * half + 2):
                        last = dve.bn_stats(stats2[:, n, :], x1_of(a, n * DIM, (n + 1) * DIM))
                last.then_inc(S("stats2_done"), 1)
                dve.wait_ge(S("stats2_done"), a + 1)
                dve.tensor_copy(carry[:], stats2[:, 0, 0:1])
                for n in range(PER_GROUP):
                    last = dve.bn_aggr(mv2[:, n, :], stats2[:, n, :])
                last.then_inc(S("mv2_done"), 1)
                dve.wait_ge(S("mv2_done"), a + 1)
                dve.wait_ge(S("ratio_parts_done"), a)
                dve.tensor_scalar(var2[:, 1, :], mv2[:, :, 1], 1.0 + RMS_EPS, RMS_EPS * LN_EPS, ALU.mult, ALU.add
                                  ).then_inc(S("var2_done"), 1)
                dve.tensor_scalar(var2[:, 0, :], mv2[:, :, 1], LN_EPS, None, ALU.add).then_inc(S("ln_var2_done"), 1)

            def x2_out(c):
                dve.wait_ge(S("wo_psum"), c + 1)
                dve.wait_ge(S("ln2_done"), c + 1)
                dve.wait_ge(S("flat_done"), c)
                dve.wait_ge(S("xs_done"), c)
                dve.tensor_tensor(x2[:].rearrange("p b c -> p (b c)"), pa[1][:], ln2[:].rearrange("p b c -> p (b c)"),
                                  ALU.add).then_inc(S("x2_done"), 1)

            def norm_2(b):
                dve.wait_ge(S("rstd2_done"), b + 1)
                dve.wait_ge(S("hnT_psum"), b)
                dve.wait_ge(S("ln2_done"), b)
                for n in range(PER_GROUP):
                    last = dve.tensor_scalar(hn[:, n, :], x1_of(b, n * DIM, (n + 1) * DIM), mv2[:, n, 0:1],
                                             rstd2[:, n:n + 1], ALU.subtract, ALU.mult)
                last.then_inc(S("hn_done"), 1)

            def ropes_k(b):
                dve.wait_ge(S("qk_psum"), 3 * b + 1)
                dve.tensor_tensor(rope_k[:].rearrange("p (b t) -> p b t", b=4),
                                  pb[1][:].rearrange("p (b t) -> p b t", b=4), per_batch(cos_sin[:]), ALU.mult
                                  ).then_inc(S("rope_done"), 1)
                dve.wait_ge(S("rope_done"), 3 * b + 1)
                dve.wait_ge(S("s_psum"), 2 * b)
                for part in (slice(0, 64), slice(64, 128)):
                    last = dve.tensor_tensor(kT[part, :], rope_k[0:64, :], rope_k[64:128, :], ALU.add)
                last.then_inc(S("qk_done"), 1)

            def ropes_q(b):
                for n in range(2):
                    dve.wait_ge(S("qk_psum"), 3 * b + n + 2)
                    dve.tensor_tensor(rope_q[:, n, :].rearrange("p (b t) -> p b t", b=4),
                                      pb[3 + n][:].rearrange("p (b t) -> p b t", b=4), per_batch((cos, sin)[n][:]),
                                      ALU.mult).then_inc(S("rope_done"), 1)
                dve.wait_ge(S("rope_done"), 3 * b + 3)
                dve.wait_ge(S("s_psum"), 2 * b)
                dve.tensor_tensor(qT[:], rope_q[:, 0, :], rope_q[:, 1, :], ALU.add).then_inc(S("qk_done"), 1)

            def maxes(b, heads):
                for h in heads:
                    dve.wait_ge(S("s_psum"), 2 * b + 1 + h // 2)
                    dve.wait_ge(S("probs_done"), 4 * b)
                    dve.tensor_reduce(neg_max[:, h, :], pb[1 + h][:].rearrange("p (b s) -> p b s", b=4), X_AXIS,
                                      ALU.max, negate=True).then_inc(S("max_done"), 1)

            def maxes_1(b):
                maxes(b, range(2))

            def maxes_2(b):
                maxes(b, range(2, HEADS))

            def probsT_out(c, heads):
                for h in heads:
                    dve.wait_ge(S("pT_psum"), 4 * c + h + 1)
                    dve.wait_ge(S("y_psum"), c)
                    dve.tensor_copy(probsT[:, h, :], pb[1 + h][:]).then_inc(S("pT_done"), 1)

            def probsT_out_1(c):
                probsT_out(c, range(2))

            def probsT_out_2(c):
                dve.wait_ge(S("probs_done"), 4 * c + 4)
                dve.reciprocal(rsum[:], prob_sums[:]).then_inc(S("rsum_done"), 1)
                probsT_out(c, range(2, HEADS - 1))
                dve.wait_ge(S("rsum_done"), c + 1)
                dve.wait_ge(S("rsumT_psum"), c)
                dve.tensor_copy(rsum_wide[:], rsum[:].unsqueeze(3).to_broadcast([128, PER_GROUP, HEADS, HEAD_DIM])
                                ).then_inc(S("rsum_wide_done"), 1)

            def yT_out(c):
                dve.wait_ge(S("y_psum"), c + 1)
                dve.wait_ge(S("rsumT_done"), c + 1)
                dve.wait_ge(S("wo_psum"), c)
                dve.tensor_tensor(yT[:], pb[0][:], rsumT[:], ALU.mult).then_inc(S("yT_done"), 1)

            def choose(d):
                dve.wait_ge(S("logits_done"), d + 1)
                dve.wait_ge(S("gates_done"), d)
                dve.tensor_copy(order2[:], logits[:, :, 0:CHOICES])
                for n in range(PER_GROUP):
                    last = dve.max(sorted8[:, n, :], logits[:, n, :])
                last.then_inc(S("sorted_done"), 1)
                dve.wait_ge(S("sorted_done"), d + 1)
                dve.wait_ge(S("numer_done"), d)
                dve.tensor_tensor(under_max[:], sorted8[:],
                                  sorted8[:, :, 0:1].to_broadcast([128, PER_GROUP, EXPERTS]), ALU.subtract
                                  ).then_inc(S("under_max_done"), 1)
                for n in range(PER_GROUP):
                    dve.max_index(order8[:, n, :], sorted8[:, n, :], logits[:, n, :]).then_inc(S("order_done"), 1)
                dve.wait_ge(S("order_done"), 4 * d + 4)
                dve.tensor_copy(order2[:], order8[:, :, 0:CHOICES]).then_inc(S("order2_done"), 1)
                dve.wait_ge(S("order2_done"), d + 1)
                dve.wait_ge(S("rank_psum"), d)
                for k in range(CHOICES):
                    last = dve.tensor_tensor(chosen[:, :, k, :],
                                             index8[:].unsqueeze(1).to_broadcast([128, PER_GROUP, EXPERTS]),
                                             order2[:, :, k:k + 1].to_broadcast([128, PER_GROUP, EXPERTS]),
                                             ALU.is_equal)
                last.then_inc(S("chosen_done"), 1)

            def gates(d):
                dve.wait_ge(S("numer_done"), d + 1)
                dve.tensor_reduce(gate_sums[:, 0, :], numer8[:], X_AXIS, ALU.add)
                dve.tensor_tensor(gate_sums[:, 1, :], numer8[:, :, 0], numer8[:, :, 1], ALU.add
                                  ).then_inc(S("gate_steps"), 1)
                dve.wait_ge(S("gate_steps"), 3 * d + 1)
                dve.scalar_tensor_tensor(gate_sums[:, 2, :], gate_sums[:, 0, :], 1e-9, gate_sums[:, 1, :],
                                         ALU.mult, ALU.add).then_inc(S("gate_steps"), 1)
                dve.wait_ge(S("gate_steps"), 3 * d + 2)
                dve.reciprocal(gate_sums[:, 0, :], gate_sums[:, 2, :]).then_inc(S("gate_steps"), 1)
                dve.wait_ge(S("gate_steps"), 3 * d + 3)
                dve.wait_ge(S("rows_free"), d)
                dve.tensor_tensor(rows[:, :, ROW_GATES:ROW_GATES + CHOICES], numer8[:, :, 0:CHOICES],
                                  gate_sums[:, 0, :].unsqueeze(2).to_broadcast([128, PER_GROUP, CHOICES]),
                                  ALU.mult).then_inc(S("gates_done"), 1)

            def slots(d):
                dve.wait_ge(S("rank_psum"), d + 1)
                dve.tensor_tensor(rank[:], pb[0][:, 0:64].rearrange("p (b l) -> p b l", b=4),
                                  list_end[:].unsqueeze(1).to_broadcast([128, PER_GROUP, LISTS]), ALU.add
                                  ).then_inc(S("slot_steps"), 1)
                dve.wait_ge(S("slot_steps"), 3 * d + 1)
                dve.tensor_tensor(rank[:], rank[:], chosen[:].rearrange("p b k e -> p b (k e)"), ALU.mult)
                dve.tensor_tensor(list_end[:], list_end[:], pb[0][:, 64:80], ALU.add).then_inc(S("slot_steps"), 1)
                dve.wait_ge(S("slot_steps"), 3 * d + 2)
                dve.tensor_reduce(slot_f[:].rearrange("p b k -> p (b k)"),
                                  rank[:].rearrange("p b (k e) -> p (b k) e", k=CHOICES), X_AXIS, ALU.add
                                  ).then_inc(S("slot_steps"), 1)
                dve.wait_ge(S("slot_steps"), 3 * d + 3)
                dve.wait_ge(S("rows_free"), d)
                dve.tensor_copy(slot[:], slot_f[:]).then_inc(S("slot_done"), 1)

            pipelined(dve, [("C", probsT_out_1), ("B", norm_2), ("C", probsT_out_2), ("A", gram_product),
                            ("Z", stats_1), ("A", ms_out), ("C", yT_out), ("B", ropes_k), ("D", choose),
                            ("B", ropes_q), ("C", x2_out), ("D", slots), ("D", gates), ("A", scale_hid_1),
                            ("B", maxes_1), ("A", scale_hid_2), ("B", maxes_2), ("Z", norm_1), ("A", x1_out)])

            steps = [0]

            def link(ins):
                steps[0] += 1
                ins.then_inc(S("table_steps"), 1)
                dve.wait_ge(S("table_steps"), steps[0])

            dve.tensor_copy(ends_i[:], list_end[0:1, :]).then_inc(S("ends_done"), 1)
            link(dve.tensor_tensor(count_f[:], list_end[:], list_base[:], ALU.subtract))
            dve.tensor_scalar(over[:], count_f[:], tile_first[:, 0:1], None, ALU.is_gt).then_inc(S("over_done"), 1)
            dve.wait_ge(S("tiles_psum"), 1)
            link(dve.tensor_copy(tiles_f[:], pa[0][:, 0:LISTS]))
            link(dve.memset(first_tile[:], 0.0))
            tiles_of = tiles_f[:].rearrange("p (k e) -> p k e", k=CHOICES)
            for e in range(EXPERTS):
                link(dve.tensor_tensor(first_tile[:, :, e + 1], first_tile[:, :, e], tiles_of[:, :, e], ALU.add))
            wide = [128, CHOICES, TABLE_COLS, EXPERTS]
            link(dve.tensor_tensor(past[:], tile_no[:].unsqueeze(3).to_broadcast(wide),
                                   first_tile[:, :, 1:].unsqueeze(2).to_broadcast(wide), ALU.is_ge))
            link(dve.tensor_reduce(expert_f[:], past[:], X_AXIS, ALU.add))
            link(dve.tensor_tensor(past[:], past[:], tiles_of.unsqueeze(2).to_broadcast(wide), ALU.mult))
            link(dve.tensor_reduce(local_f[:], past[:], X_AXIS, ALU.add))
            link(dve.tensor_tensor(local_f[:], tile_no[:], local_f[:], ALU.subtract))
            link(dve.tensor_scalar(used_f[:], expert_f[:], EXPERTS - 0.5, None, ALU.is_lt))
            link(dve.scalar_tensor_tensor(local_f[:], local_f[:], 128.0, choice_row[:], ALU.mult, ALU.add))
            link(dve.scalar_tensor_tensor(local_f[:], expert_f[:], float(LIST_ROWS), local_f[:], ALU.mult, ALU.add))
            link(dve.tensor_tensor(unused_f[:], tile_no[:],
                                   first_tile[:, :, EXPERTS:].to_broadcast([128, CHOICES, TABLE_COLS]), ALU.subtract))
            link(dve.scalar_tensor_tensor(unused_f[:], unused_f[:], 128.0, choice_pad[:], ALU.mult, ALU.add))
            link(dve.tensor_tensor(local_f[:], local_f[:], unused_f[:], ALU.subtract))
            link(dve.tensor_tensor(local_f[:], local_f[:], used_f[:], ALU.mult))
            dve.tensor_tensor(table_cols[:, 0, :, :], local_f[:], unused_f[:], ALU.add)
            link(dve.tensor_tensor(table_cols[:, 1, :, :], expert_f[:], used_f[:], ALU.mult))
            dve.tensor_tensor(table_diag.rearrange("p h (c n) -> p (h c) n", n=128),
                              ident[:].unsqueeze(1).to_broadcast([128, 2 * CHOICES * TABLE_COLS, 128]),
                              table_cols[:].rearrange("p t k c -> p (t k c)").unsqueeze(2).to_broadcast(
                                  [128, 2 * CHOICES * TABLE_COLS, 128]), ALU.mult).then_inc(S("table_diag_done"), 1)
            for n, table in enumerate((tile_row, tile_expert)):
                dve.wait_ge(S("table_psum"), n + 1)
                dve.tensor_copy(table[:].rearrange("p (k n) -> p k n", k=CHOICES),
                                pb[n][0:1, :].rearrange("p (k n) -> p k n", k=CHOICES)[:, :, 0:TILES_PER_CHOICE]
                                ).then_inc(S("tables_done"), 1)

            def expert(n, u):
                dve.wait_ge(S("g_done"), n + 1)
                dve.wait_ge(S("u_psum"), n + 1)
                if since(n, 2):
                    dve.wait_ge(S("hhT_psum"), n - 1)
                dve.tensor_tensor(hh[:, u % 2, :], pb[2 + u % 2][:, 0:HID], act_g[:, u % 2, :], ALU.mult
                                  ).then_inc(S("hh_done"), 1)

            def scale_out(n, u, turn, choice):
                dve.wait_ge(S("e_psum"), n + 1)
                if since(n, UNROLL):
                    dve.wait_ge(added[u], 16 * turn)
                gate = ROW_GATES + choice
                dve.tensor_scalar(expert_out[:, u, :], (pb[4], pa[2])[u % 2][:, 0:DIM], tile_in[:, u, gate:gate + 1],
                                  None, ALU.mult).then_inc(S("scaled"), 1)
                dve.tensor_copy(token[:, u:u + 1], tile_in[:, u, ROW_TOKEN:ROW_TOKEN + 1]
                                ).then_inc(S("token_done"), 1)

            def turn(i, choice):
                for u in range(UNROLL):
                    n = UNROLL * i + u
                    expert(n, u)
                    if u >= 2:
                        scale_out(n - 2, u - 2, i, choice)
                    elif since(n, 2):
                        scale_out(n - 2, u - 2 + UNROLL, i - 1, 0 if isinstance(i, int) and i <= TURNS else choice)
            turn(0, 0)
            with dve.Fori(1, TURNS) as i:
                turn(i, 0)
            turn(TURNS, 1)
            with dve.Fori(TURNS + 1, 2 * TURNS) as i:
                turn(i, 1)
            for u in range(UNROLL - 2, UNROLL):
                scale_out(TILES - UNROLL + u, u, 2 * TURNS - 1, 1)

        @block.tensor
        def _(pe):
            pe.wait_ge(weights_in, 16 * len(WEIGHTS))
            pe.wait_ge(consts_in, 16 * len(CONSTS))
            pe.wait_ge(S("pool_prep"), 1)
            pe.wait_ge(S("prep"), 1)

            def cols(n):
                return slice(n * 128, (n + 1) * 128)

            for c in range(GNN_CHUNKS):
                pe.matmul(pa[0][:, 0:128], w1gT[:, c, :], w1gT[:, c, :], start=(c == 0), stop=(c == GNN_CHUNKS - 1))
            for c in range(GNN_CHUNKS):
                pe.matmul(pa[1][:, 0:1], w1gT[:, c, :], b1g[:, c:c + 1], start=(c == 0), stop=(c == GNN_CHUNKS - 1))
            pe.matmul(pa[2][:, 0:GNN_CHUNKS], ones[:], b1g_sq[:], start=True, stop=True).then_inc(S("gram_psum"), 1)
            pe.wait_ge(S("prep"), 4)

            def aggregate(a):
                pe.wait_ge(S("ln1_done"), a + 1)
                pe.wait_ge(S("adj_ready"), a + 1)
                pe.wait_ge(S("rrms_cols_done"), a)
                for n in range(PER_GROUP):
                    last = pe.matmul(pa[2][:, cols(n)], ln1[:, n, :], adj_eps[:, n, :], start=True, stop=True)
                last.then_inc(S("agg_psum"), 1)

            def project(c):
                pe.wait_ge(S("yT_done"), c + 1)
                for n in range(PER_GROUP):
                    last = pe.matmul(pa[1][:, cols(n)], yT[:, cols(n)], wo[:], start=True, stop=True)
                last.then_inc(S("wo_psum"), 1)

            def gram_aggregate(a):
                pe.wait_ge(S("agg_done"), a + 1)
                pe.wait_ge(S("x1_done"), 2 * a)
                pe.matmul(pa[0][:], gram[:], agg[:], start=True, stop=True).then_inc(S("gram_agg_psum"), 1)

            def mean_square(a):
                pe.wait_ge(S("gram_product_done"), a + 1)
                for n in range(PER_GROUP):
                    last = pe.transpose(pa[2][:, cols(n)], agg_gram[:, cols(n)], ident[:])
                last.then_inc(S("ms_psum"), 1)

            def spread(a, d):
                pe.wait_ge(S("rrms_wide_done"), a + 1)
                pe.wait_ge(S("ms_done"), a + 1)
                if d is not None:
                    pe.wait_ge(S("logits_done"), d + 1)
                for n in range(PER_GROUP):
                    last = pe.transpose(pa[2][:, cols(n)], rrms_wide[:, n, :], ident[:])
                last.then_inc(S("rrms_psum"), 1)

            def hidden_1(a, c):
                if c is not None:
                    pe.wait_ge(S("rsumT_done"), c + 1)
                for n in range(2):
                    if n and c is not None:
                        pe.wait_ge(S("x2_done"), c + 1)
                    pe.matmul(pa[n][:], w1g[:, cols(n)], agg[:], start=True, stop=True).then_inc(S("hid_psum"), 1)

            def hidden_2(a):
                for c in range(2, 4):
                    pe.wait_ge(S("scaled_done"), 4 * a + c - 1)
                    pe.matmul(pa[c % 2][:], w1g[:, cols(c)], agg[:], start=True, stop=True).then_inc(S("hid_psum"), 1)

            def gnn_out(a):
                pe.wait_ge(S("silu_done"), 4 * a + 4)
                for n in range(PER_GROUP):
                    for c in range(GNN_CHUNKS):
                        last = pe.matmul(pa[n // 2][:, cols(n % 2)], hid[:, c, cols(n)], w2g[:, c, :],
                                         start=(c == 0), stop=(c == GNN_CHUNKS - 1))
                    if n % 2:
                        last.then_inc(S("gnn_psum"), 1)

            def hn_turn(b, c):
                pe.wait_ge(S("hn_done"), b + 1)
                if c is not None:
                    pe.wait_ge(S("pT_done"), 3 * c + 1)
                for n in range(PER_GROUP):
                    last = pe.transpose(pb[1][:, cols(n)], hn[:, n, :], ident[:])
                last.then_inc(S("hnT_psum"), 1)

            def keys(b):
                pe.wait_ge(S("hnT_done"), b + 1)
                pe.matmul(pb[1][:], wk[:].rearrange("p r g d -> p (r g d)"), hnT[:], start=True, stop=True
                          ).then_inc(S("qk_psum"), 1)

            def queries_values(b, c):
                for n, w in enumerate((wq, wq_rot)):
                    pe.matmul(pb[3 + n][:], w[:].rearrange("p h d -> p (h d)"), hnT[:], start=True,
                              stop=True).then_inc(S("qk_psum"), 1)
                if c is not None:
                    pe.wait_ge(S("yT_done"), c + 1)
                for n in range(PER_GROUP):
                    last = pe.matmul(pb[0][:, 64 * n:64 * n + 64], hnT[:, cols(n)], wv[:], start=True, stop=True)
                last.then_inc(S("v_psum"), 1)

            def scores(b, half):
                pe.wait_ge(S("qk_done"), 2 * b + 2)
                heads = range(2 * half, 2 * half + 2)
                for h in heads:
                    pe.matmul(pb[1 + h][:], ident_bf[:], mask_rows[:], start=True, stop=False)
                for n in range(PER_GROUP):
                    for h in heads:
                        part = slice(32 * h, 32 * h + 32)
                        last = pe.matmul(pb[1 + h][:, cols(n)], qT[part, cols(n)], kT[part, cols(n)], start=False,
                                         stop=(n == 3))
                last.then_inc(S("s_psum"), 1)

            def scores_1(b):
                scores(b, 0)

            def scores_2(b):
                scores(b, 1)

            def probs_turn(c, heads):
                for h in heads:
                    pe.wait_ge(S("probs_done"), 4 * c + h + 1)
                    for n in range(PER_GROUP):
                        last = pe.transpose(pb[1 + h][:, cols(n)], probs[:, h, cols(n)], ident[:])
                    last.then_inc(S("pT_psum"), 1)

            def probs_turn_1(c):
                probs_turn(c, range(3))

            def probs_turn_2(c):
                probs_turn(c, range(3, HEADS))

            def attend(c, d):
                pe.wait_ge(S("pT_done"), 3 * c + 3)
                pe.wait_ge(S("pT_last_done"), c + 1)
                pe.wait_ge(S("v_done"), c + 1)
                if d is not None:
                    pe.wait_ge(S("slot_done"), d)
                for n in range(PER_GROUP):
                    for h in range(HEADS):
                        last = pe.matmul(pb[0][32 * h:32 * h + 32, cols(n)], v[:, n, h % KV_HEADS, :],
                                         probsT[:, h, cols(n)], start=True, stop=True)
                last.then_inc(S("y_psum"), 1)

            def rsum_turn(c, a):
                if a is not None:
                    pe.wait_ge(S("gram_product_done"), a + 1)
                pe.wait_ge(S("rsum_wide_done"), c + 1)
                for n in range(PER_GROUP):
                    last = pe.transpose(pa[0][:, cols(n)], rsum_wide[:, n, :, :].rearrange("p h d -> p (h d)"),
                                        ident[:])
                last.then_inc(S("rsumT_psum"), 1)

            def flat_turn(d):
                pe.wait_ge(S("flat_done"), d + 1)
                pe.wait_ge(S("flT_done"), d)
                for n in range(PER_GROUP):
                    last = pe.transpose(pb[3][:, cols(n)], rows[:, n, 0:DIM], ident[:])
                last.then_inc(S("flT_psum"), 1)

            def router(d, a):
                pe.wait_ge(S("flT_done"), d + 1)
                pe.wait_ge(S("logits_done"), d)
                if a is not None:
                    pe.wait_ge(S("ms_done"), a + 1)
                for n in range(PER_GROUP):
                    last = pe.matmul(pa[2][:, 8 * n:8 * n + 8], flT[:, cols(n)], wr[:], start=True, stop=True)
                last.then_inc(S("router_psum"), 1)

            def ranks(d, b):
                pe.wait_ge(S("chosen_done"), d + 1)
                pe.wait_ge(S("slot_done"), d)
                if b is not None:
                    pe.wait_ge(S("v_done"), b + 1)
                of = [chosen[:, n, :, :].rearrange("p k e -> p (k e)") for n in range(PER_GROUP)]
                for n in range(PER_GROUP + 1):
                    out = pb[0][:, LISTS * n:LISTS * (n + 1)]
                    terms = [(ones_bf, of[m]) for m in range(n)] + [(before_bf, of[n]) for _ in range(n < PER_GROUP)]
                    for m, (rows_of, ones_of) in enumerate(terms):
                        last = pe.matmul(out, rows_of[:], ones_of, start=(m == 0), stop=(m == len(terms) - 1))
                last.then_inc(S("rank_psum"), 1)

            pipelined(pe, [("A", aggregate), ("C", probs_turn_1), ("A", gram_aggregate), ("C", probs_turn_2),
                           ("Bc", hn_turn), ("Cd", attend), ("Ca", rsum_turn), ("A", mean_square), ("D", flat_turn),
                           ("B", keys), ("Da", router), ("Bc", queries_values), ("C", project), ("Db", ranks),
                           ("Ad", spread), ("Ac", hidden_1), ("B", scores_1), ("A", hidden_2), ("B", scores_2),
                           ("A", gnn_out)])

            pe.wait_ge(S("over_done"), 1)
            pe.matmul(pa[0][:, 0:LISTS], ones[:], over[:], start=True, stop=True).then_inc(S("tiles_psum"), 1)
            pe.wait_ge(S("table_diag_done"), 1)
            for n in range(2):
                pe.matmul(pb[n][0:1, :], ones[:, 0:1], table_diag[:, n, :], start=True, stop=True
                          ).then_inc(S("table_psum"), 1)
            pe.wait_ge(S("experts_scaled"), 1)
            pe.wait_ge(S("tables_done"), CHOICES)
            pe.wait_ge(S("logits_done"), GROUPS)
            pe.wait_ge(S("slot_done"), GROUPS)

            def expert_of(n):
                return pe.value_load(tile_expert[0:1, bass.ds(n, 1)], min_val=0, max_val=EXPERTS - 1)

            def up(n, u, e):
                pe.wait_ge(S("tokT_done"), n + 1)
                if since(n, 2):
                    pe.wait_ge(S("g_done"), n - 1)
                pe.matmul(pb[u % 2][:, 0:HID], tokT[:, u % 2, :], w1e[:, bass.ds(e, 1), :]
                          .rearrange("p e n -> p (e n)"), start=True, stop=True).then_inc(S("g_psum"), 1)
                if since(n, 2):
                    pe.wait_ge(S("hh_done"), n - 1)
                pe.matmul(pb[2 + u % 2][:, 0:HID], tokT[:, u % 2, :], w3e[:, bass.ds(e, 1), :]
                          .rearrange("p e n -> p (e n)"), start=True, stop=True).then_inc(S("u_psum"), 1)

            def down(n, u, e):
                pe.wait_ge(S("hhT_done"), n + 1)
                if since(n, 2):
                    pe.wait_ge(S("scaled"), n - 1)
                for c, (lo, m) in enumerate(HID_CHUNKS):
                    last = pe.matmul((pb[4], pa[2])[u % 2][:, 0:DIM], hhT[0:m, u % 2, c, :],
                                     w2e[0:m, bass.ds(e, 1), c, :].rearrange("p e n -> p (e n)"),
                                     start=(c == 0), stop=(c == 2))
                last.then_inc(S("e_psum"), 1)

            def token_turn(n, u, turn):
                pe.wait_ge(tile_loaded[u], 16 * turn + 16)
                if since(n, 1):
                    pe.wait_ge(S("tokT_done"), n)
                pe.transpose(pa[0][:, 0:128], tile_in[:, u, 0:DIM], ident[:]).then_inc(S("tokT_psum"), 1)

            def hidden_turn(n, u):
                pe.wait_ge(S("hh_done"), n + 1)
                if since(n, 1):
                    pe.wait_ge(S("hhT_done"), n)
                for c, (lo, m) in enumerate(HID_CHUNKS):
                    last = pe.transpose(pa[1][0:m, cols(c)], hh[:, u % 2, lo:lo + m], ident[:])
                last.then_inc(S("hhT_psum"), 1)

            carried = [nc.alloc_registers(f"carried_expert{k}", engines=[pe.engine]) for k in range(3)]

            def turn(i):
                first = isinstance(i, int) and i == 0
                if first:
                    experts = [None, None, expert_of(0)]
                else:
                    experts = [nc.snap(registers, min_val=0, max_val=EXPERTS - 1) for registers in carried]
                for u in range(UNROLL):
                    n = UNROLL * i + u
                    up(n, u, experts[u + 2])
                    if not (isinstance(n, int) and n == TILES - 1):
                        token_turn(n + 1, (u + 1) % UNROLL, i + (u + 1) // UNROLL)
                        experts.append(expert_of(n + 1))
                    if since(n, 1):
                        hidden_turn(n - 1, u + 1)
                    if since(n, 2):
                        down(n - 2, u, experts[u])
                for registers, expert in zip(carried, experts[UNROLL:]):
                    nc.regs_mov(registers, expert)
                return experts
            token_turn(0, 0, 0)
            turn(0)
            with pe.Fori(1, 2 * TURNS - 1) as i:
                turn(i)
            last_experts = turn(2 * TURNS - 1)
            hidden_turn(TILES - 1, 1)
            down(TILES - 2, 0, last_experts[UNROLL])
            down(TILES - 1, 1, last_experts[UNROLL + 1])


def tables():
    inv_freq = 1.0 / 10000.0 ** (np.arange(0, HEAD_DIM, 2, dtype=np.float32) / HEAD_DIM)
    freqs = np.outer(np.arange(TOKENS, dtype=np.float32), inv_freq)
    emb = np.concatenate([freqs, freqs], axis=-1).astype(np.float32)
    later = np.arange(TOKENS)[None, :] > np.arange(TOKENS)[:, None]
    mask = np.where(later, MASKED, 0.0)
    before = np.zeros((128, COLS))
    before[:, 0:128] = np.arange(128)[:, None] < np.arange(128)[None, :]
    partition = np.arange(128, dtype=np.float32)

    def table_layout(values):
        return np.broadcast_to(values, (128, CHOICES, TABLE_COLS)).astype(np.float32)

    pad_tail = np.zeros((128, DUMPS, ROW - DIM), np.float32)
    pad_tail[:, :, ROW_TOKEN - DIM] = ALL_TOKENS + 128 * np.arange(DUMPS)[None, :] + partition[:, None]
    first_tokens = np.zeros((128, PER_GROUP, ROW - ROW_TOKEN), np.float32)
    first_tokens[:, :, 0] = 128 * np.arange(PER_GROUP)[None, :] + partition[:, None]
    return {
        "ident": np.eye(128, dtype=np.float32),
        "narrow": np.stack([np.tile(mask, (1, PER_GROUP)), before], axis=1).astype(np.float32),
        "cos": np.tile(np.cos(emb).T, (HEADS, 1)).astype(np.float32),
        "sin": np.tile(np.sin(emb).T, (HEADS, 1)).astype(np.float32),
        "cos_sin": np.concatenate([np.tile(table(emb).T, (KV_HEADS, 1)) for table in (np.cos, np.sin)]
                                  ).astype(np.float32),
        "index8": np.tile(np.arange(EXPERTS, dtype=np.float32), (128, 1)),
        "list_base": np.tile(LIST_ROWS * np.arange(LISTS, dtype=np.float32), (128, 1)),
        "tile_no": table_layout(128 * np.arange(TABLE_COLS)[None, None, :] + partition[:, None, None]),
        "tile_first": 128 * partition[:, None],
        "choice_row": table_layout(EXPERTS * LIST_ROWS * np.arange(CHOICES)[None, :, None]),
        "choice_pad": table_layout(PAD_ROW + 128 * (UNUSED // 2) * np.arange(CHOICES)[None, :, None]),
        "pad_tail": pad_tail,
        "first_tokens": first_tokens,
    }


def kernel(**inputs):
    import concourse.bacc as bacc
    from concourse.bass_utils import run_bass_kernel_spmd

    def arr(name):
        return np.asarray(inputs[name])

    def grouped(a):
        return a.reshape(GROUPS, PER_GROUP, 128, 128)

    w2 = np.zeros((128, EXPERTS, 3, DIM), np.float32)
    for c, (lo, m) in enumerate(HID_CHUNKS):
        w2[:m, :, c, :] = arr("L0_ffn_w2")[:, :, lo:lo + m].transpose(2, 0, 1)
    laid = {
        "x": grouped(arr("x")).transpose(0, 2, 1, 3),
        "adj": grouped(arr("adj")).transpose(0, 3, 1, 2),
        "w1g": arr("L0_gnn_W1"),
        "w1gT": arr("L0_gnn_W1").T.reshape(GNN_CHUNKS, 128, DIM).transpose(1, 0, 2),
        "b1g": arr("L0_gnn_b1").reshape(GNN_CHUNKS, 128).T,
        "rmsw": arr("L0_gnn_rms_weight").reshape(GNN_CHUNKS, 128).T,
        "w2g": arr("L0_gnn_W2").reshape(GNN_CHUNKS, 128, DIM).transpose(1, 0, 2),
        "b2g": np.broadcast_to(arr("L0_gnn_b2"), (128, DIM)),
        "eps": np.broadcast_to(arr("L0_gnn_epsilon"), (128, 1)),
        "norm1": arr("L0_ffn_ln1_w").reshape(DIM, 1),
        "norm2": arr("L0_ffn_ln2_w").reshape(DIM, 1),
        "wq": arr("L0_ffn_wq").T.reshape(DIM, HEADS, HEAD_DIM)[:, HEAD_ORDER],
        "wk": arr("L0_ffn_wk").T.reshape(DIM, KV_HEADS, HEAD_DIM),
        "wv": arr("L0_ffn_wv").T,
        "wo": arr("L0_ffn_wo").T.reshape(HEADS, HEAD_DIM, DIM)[HEAD_ORDER].reshape(DIM, DIM),
        "wr": arr("L0_ffn_router_w").T,
        "w1e": arr("L0_ffn_w1").transpose(2, 0, 1),
        "w3e": arr("L0_ffn_w3").transpose(2, 0, 1),
        "w2e": w2,
    }
    laid.update(tables())

    nc = bacc.Bacc("TRN2", target_bir_lowering=False, num_devices=1)
    arrays, t = {}, {}
    for name, a in laid.items():
        a = np.ascontiguousarray(a)
        arrays[f"in_{name}"] = a
        t[name] = nc.dram_tensor(f"in_{name}", a.shape, mybir.dt.from_np(a.dtype), kind="ExternalInput").ap()
    t["out"] = nc.dram_tensor("out", (ALL_TOKENS + 128 * DUMPS, DIM), F32, kind="ExternalOutput").ap()
    t["sorted"] = nc.dram_tensor("sorted", (SORTED_ROWS, ROW), F32, kind="Internal").ap()
    gnn_attention_moe(nc, t)
    r = run_bass_kernel_spmd(nc, [arrays], core_ids=[0])
    out = r.results[0]["out"]
    return out[:ALL_TOKENS].reshape(BATCHES, TOKENS, DIM)
```
